# Optimizing a Trainium2 kernel written in Bass

```python
import numpy as np
import jax
import jax.numpy as jnp

def _softmax(x, axis=-1):
    return jax.nn.softmax(x, axis=axis)
def _gelu(x):
    return jax.nn.gelu(x, approximate=True)
def _silu(x):
    return jax.nn.silu(x)
def _sigmoid(x):
    return jax.nn.sigmoid(x)
def _layernorm(x, axis=-1, eps=1e-5):
    m = jnp.mean(x, axis=axis, keepdims=True)
    v = jnp.var(x, axis=axis, keepdims=True)
    return (x - m) / jnp.sqrt(v + eps)
def _scatter_add(tgt, idx, src, axis=0):
    return tgt.at[idx].add(src)
def _segment_sum(src, seg, n):
    return jax.ops.segment_sum(src, seg, n)

kernel_name = 'mk_adj_resnorm_d1_adj_512_66fe6e'

def setup_inputs(seed: int = 0):
    np.random.seed(seed)
    _w = jnp.asarray
    def _rec_inputs():
        import jax
        import jax.numpy as jnp
        _gk = jax.random.key(seed)
        x = 7.22e-05 + 1 * jax.random.normal(jax.random.fold_in(_gk, 1), (128, 128, 512), jnp.float32)
        _a = jax.random.bernoulli(jax.random.fold_in(_gk, 2), 0.03125, (128, 128, 128))
        _a = jnp.logical_or(_a, jnp.swapaxes(_a, -1, -2))
        _a = jnp.logical_or(_a, jnp.eye(128, dtype=bool))
        _af = _a.astype(jnp.float32)
        _af = _af * jax.random.uniform(jax.random.fold_in(_gk, 3), (128, 128, 128), jnp.float32, 0.05, 1)
        adj = _af
        return x, adj
    x, adj = _rec_inputs()
    def _L0_gnn_setup():
        import jax, jax.numpy as jnp
        import numpy as np
        EPS_LN = 1e-05

        def hypergraph_conv(x, adj, W, b):
            N, C, _ = adj.shape
            H = (adj != 0).astype(x.dtype)
            w = adj.reshape(N, -1)[:, :C]
            xw = jnp.einsum('ncd,hd->nch', x, W)
            Dn = jnp.einsum('nce,ne->nc', H, w)
            Dn = jnp.where(Dn > 0, 1.0 / Dn, 0.0)
            Be = H.sum(axis=1)
            Be = jnp.where(Be > 0, 1.0 / Be, 0.0)
            m = Be[:, :, None] * jnp.einsum('nce,nch->neh', H, xw)
            out = Dn[:, :, None] * jnp.einsum('nce,neh->nch', H, m)
            return out + b

        def layer_norm(x, g, b):
            mu = jnp.mean(x, axis=-1, keepdims=True)
            var = jnp.var(x, axis=-1, keepdims=True)
            return (x - mu) * jax.lax.rsqrt(var + EPS_LN) * g + b
        key = jax.random.key(seed)
        ks = jax.random.split(key, 4)
        N, C, Din, Dh, Dout = (16, 1024, 512, 1024, 512)
        x = jax.random.normal(ks[0], (N, C, Din), dtype=jnp.float32)
        adj = jax.random.uniform(ks[1], (N, C, C), dtype=jnp.float32, minval=0.1, maxval=1.0)
        W1 = jax.random.normal(ks[2], (Dh, Din), dtype=jnp.float32) * (1.0 / np.sqrt(Din))
        b1 = jnp.zeros((Dh,), dtype=jnp.float32)
        gamma = jnp.ones((Dh,), dtype=jnp.float32)
        beta = jnp.zeros((Dh,), dtype=jnp.float32)
        W2 = jax.random.normal(ks[3], (Dout, Dh), dtype=jnp.float32) * (1.0 / np.sqrt(Dh))
        b2 = jnp.zeros((Dout,), dtype=jnp.float32)
        return {'x': x, 'adj': adj, 'W1': W1, 'b1': b1, 'gamma': gamma, 'beta': beta, 'W2': W2, 'b2': b2}
    _L0_gnn_all = _L0_gnn_setup()
    _L0_gnn_in = {k: v for k, v in _L0_gnn_all.items() if k in ('W1', 'b1', 'gamma', 'beta', 'W2', 'b2', )}
    del _L0_gnn_all

    return {
        "x": x,
        "adj": adj,
        "L0_gnn_W1": _L0_gnn_in["W1"],
        "L0_gnn_b1": _L0_gnn_in["b1"],
        "L0_gnn_gamma": _L0_gnn_in["gamma"],
        "L0_gnn_beta": _L0_gnn_in["beta"],
        "L0_gnn_W2": _L0_gnn_in["W2"],
        "L0_gnn_b2": _L0_gnn_in["b2"],
    }

def reference(x, adj, L0_gnn_W1, L0_gnn_b1, L0_gnn_gamma, L0_gnn_beta, L0_gnn_W2, L0_gnn_b2):
    import jax
    import jax.numpy as jnp
    def _L0_gnn_ref(x, adj, W1, b1, gamma, beta, W2, b2):
        import jax, jax.numpy as jnp
        import numpy as np
        EPS_LN = 1e-05

        def hypergraph_conv(x, adj, W, b):
            N, C, _ = adj.shape
            H = (adj != 0).astype(x.dtype)
            w = adj.reshape(N, -1)[:, :C]
            xw = jnp.einsum('ncd,hd->nch', x, W)
            Dn = jnp.einsum('nce,ne->nc', H, w)
            Dn = jnp.where(Dn > 0, 1.0 / Dn, 0.0)
            Be = H.sum(axis=1)
            Be = jnp.where(Be > 0, 1.0 / Be, 0.0)
            m = Be[:, :, None] * jnp.einsum('nce,nch->neh', H, xw)
            out = Dn[:, :, None] * jnp.einsum('nce,neh->nch', H, m)
            return out + b

        def layer_norm(x, g, b):
            mu = jnp.mean(x, axis=-1, keepdims=True)
            var = jnp.var(x, axis=-1, keepdims=True)
            return (x - mu) * jax.lax.rsqrt(var + EPS_LN) * g + b
        h = jax.nn.relu(hypergraph_conv(x, adj, W1, b1))
        h = layer_norm(h, gamma, beta)
        y = hypergraph_conv(h, adj, W2, b2)
        return y + x

    x = _layernorm(x + _L0_gnn_ref(x, adj, L0_gnn_W1, L0_gnn_b1, L0_gnn_gamma, L0_gnn_beta, L0_gnn_W2, L0_gnn_b2), axis=-1)
    return x


_drawn_inputs = setup_inputs


def setup_inputs(seed=0):
    import zlib

    import numpy as np

    out = dict(_drawn_inputs(seed))
    spreads = {'L0_gnn_b1': (0.0, 0.1),
     'L0_gnn_gamma': (1.0, 0.2),
     'L0_gnn_beta': (0.0, 0.1),
     'L0_gnn_b2': (0.0, 0.1)}
    factors = {}
    for name, (base, spread) in spreads.items():
        noise = np.random.default_rng([zlib.crc32(name.encode()), seed]).standard_normal(out[name].shape)
        drawn = base * np.exp(spread * noise) if base else spread * noise
        out[name] = jnp.asarray(drawn.astype(out[name].dtype))
    for name, factor in factors.items():
        out[name] = (out[name] * factor).astype(out[name].dtype)
    return out
```

```python
from contextlib import ExitStack

import concourse.bass as bass
from concourse import mybir

F32 = mybir.dt.float32
F32R = mybir.dt.float32r
ALU = mybir.AluOpType
ACT = mybir.ActivationFunctionType
AX = mybir.AxisListType

P = 128
GB = 4
COLS = GB * P
EPS = 1e-5
TINY = 1.2e-38


def adj_resnorm_kernel(nc, x, adj, w1t, b1, gamma, beta, w2t, b2, out):
    N, C, DI = x.shape
    DH = w1t.shape[1]
    assert C == P and N % GB == 0 and DI == COLS and w2t.shape == (DH, DI)
    NB = N // GB
    DT = DI // P
    HT = DH // P
    MAIN = 3
    assert (HT + GB) % MAIN == 0 and HT >= 8 and DT == 4 and GB == 4

    x_v = x.rearrange("(n g) c d -> n c g d", g=GB)
    adj_v = adj.rearrange("(n g) c e -> n c g e", g=GB)
    w_v = adj[:, 0, :].rearrange("(n g) e -> n g e", g=GB)
    out_v = out.rearrange("(n g) c d -> n c g d", g=GB)
    w1_v = w1t.rearrange("(t p) h -> p t h", p=P)
    w2_v = w2t.rearrange("(t p) d -> p t d", p=P)

    with ExitStack() as ctx:
        def sb(name, shape, dt=F32):
            return ctx.enter_context(nc.sbuf_tensor(name, shape, dt))

        def bank(name):
            return ctx.enter_context(nc.psum_tensor(name, [P, COLS], F32))

        def sem(name):
            return ctx.enter_context(nc.semaphore(name))

        w1h = sb("w1h", [P, DT, DH], F32R)
        w1l = sb("w1l", [P, DT, DH], F32R)
        w2h = sb("w2h", [P, HT, DI], F32R)
        w2l = sb("w2l", [P, HT, DI], F32R)
        ident = sb("ident", [P, P])
        ones = sb("ones", [P, P])
        pick = sb("pick", [P, 2, P])
        b1c = sb("b1c", [P, HT])
        gammac = sb("gammac", [P, HT])
        betac = sb("betac", [P, HT])
        b2b = sb("b2b", [P, DI])
        wbb = sb("wbb", [P, DI])
        neghalf = sb("neghalf", [P, GB])
        adj_sb = sb("adj_sb", [P, GB, P])
        wrow = sb("wrow", [P, GB, P])
        x_sb = sb("x_sb", [P, GB, DI])
        hw = sb("hw", [P, GB, P])
        dnh = sb("dnh", [P, GB, P])
        ht_sb = sb("ht_sb", [P, GB, P])
        beht = sb("beht", [P, GB, P])
        dnht = sb("dnht", [P, GB, P])
        gt = sb("gt", [P, GB, P])
        gth = sb("gth", [P, GB, P], F32R)
        gtl = sb("gtl", [P, GB, P], F32R)
        small = sb("small", [P, 18, GB])
        ath = sb("ath", [P, DT, COLS], F32R)
        atl = sb("atl", [P, DT, COLS], F32R)
        rr = sb("rr", [P, HT, COLS])
        rh = sb("rh", [P, HT, COLS], F32R)
        rl = sb("rl", [P, HT, COLS], F32R)
        QS = 4
        rq = sb("rq", [P, QS, COLS])
        sums = sb("sums", [P, 2, COLS])
        ys = sb("ys", [P, 2, DI])
        yh = sb("yh", [P, 2, DI], F32R)
        yl = sb("yl", [P, 2, DI], F32R)
        resid = sb("resid", [P, GB, DI])
        t_sb = sb("t_sb", [P, GB, DI])
        bns = sb("bns", [P, GB, 6])

        p_main = [bank(f"p_main{i}") for i in range(MAIN)]
        p_at = [bank(f"p_at{i}") for i in range(2)]
        p_prep, p_agg, p_stat = bank("p_prep"), bank("p_agg"), bank("p_stat")
        prep4 = p_prep[:].rearrange("p (g c) -> p g c", g=GB)
        stat4 = p_stat[:].rearrange("p (g c) -> p g c", g=GB)

        dsum, dpos, dsafe, drec, dn = (small[:, i] for i in range(5))
        deg, bpos, bsafe, brec, be = (small[:, i] for i in range(5, 10))
        mean1, msq1, var1, rstd1, mean2, diff2, var2, rstd2 = (small[:, i] for i in range(10, 18))

        w1_stage = [resid[:].rearrange("p g d -> p (g d)").rearrange("p (t h) -> p t h", h=DH),
                    t_sb[:].rearrange("p g d -> p (g d)").rearrange("p (t h) -> p t h", h=DH)]
        w2_stage = rr
        beta_rep = sums[:].rearrange("p a d -> p (a d)").rearrange("p (t c) -> p t c", c=P)
        gamma_rep = ys[:].rearrange("p a d -> p (a d)").rearrange("p (t c) -> p t c", c=P)

        consts_loaded, w1_loaded, w2_loaded = sem("consts_loaded"), sem("w1_loaded"), sem("w2_loaded")
        adj_loaded, wrow_loaded, x_loaded, stored = sem("adj_loaded"), sem("wrow_loaded"), sem("x_loaded"), sem("stored")
        zeroed, zeroed_ident, made = sem("zeroed"), sem("zeroed_ident"), sem("made")
        w1h_ready, w1_ready = sem("w1h_ready"), sem("w1_ready")
        rep_ready, w2sums_done, w2c_ready, w2h_ready, w2_ready = (
            sem(n) for n in ("rep_ready", "w2sums_done", "w2c_ready", "w2h_ready", "w2_ready"))
        adjt_done, dnht_done, gt_done, at_done = sem("adjt_done"), sem("dnht_done"), sem("gt_done"), sem("at_done")
        z_done, y_done, stats_done, agg_done = sem("z_done"), sem("y_done"), sem("stats_done"), sem("agg_done")
        rh_ready, r_ready, q_ready = sem("rh_ready"), sem("r_ready"), sem("q_ready")
        dnht_ready, gt_ready, gth_ready, ath_ready, yh_ready = (
            sem(n) for n in ("dnht_ready", "gt_ready", "gth_ready", "ath_ready", "yh_ready"))
        dnorm, dnh_ready, ht_ready, benorm, beht_ready = (
            sem(n) for n in ("dnorm", "dnh_ready", "ht_ready", "benorm", "beht_ready"))
        gtl_ready, atl_ready, rl_ready, resid_ready = (
            sem(n) for n in ("gtl_ready", "atl_ready", "rl_ready", "resid_ready"))
        var1_steps, ys_ready, yl_ready, t_ready, bns_ready, var2_steps, norm_ready = (
            sem(n) for n in ("var1_steps", "ys_ready", "yl_ready", "t_ready", "bns_ready", "var2_steps", "norm_ready"))
        sum_steps, rstd1_ready, rstd2_ready = (
            sem(n) for n in ("sum_steps", "rstd1_ready", "rstd2_ready"))

        block = ctx.enter_context(nc.Block())

        DN_STEPS, BE_STEPS, VAR1_STEPS, VAR2_STEPS = 6, 5, 5, 7
        SUM_STEPS = 2 * (HT - 1)

        def batches(eng, body):
            body(0, True, False)
            with eng.Fori(1, NB - 1) as b:
                body(b, False, False)
            body(NB - 1, False, True)

        @block.sync
        def _(sp):
            def load_adj(b):
                sp.dma_start(adj_sb[:], adj_v[b]).then_inc(adj_loaded, 16)
                sp.dma_start(wrow[:], w_v[b].partition_broadcast(P)).then_inc(wrow_loaded, 16)

            load_adj(0)
            sp.dma_start(x_sb[:], x_v[0]).then_inc(x_loaded, 16)
            for i in range(2):
                sp.dma_start(w1_stage[i], w1_v[:, 2 * i:2 * i + 2]).then_inc(w1_loaded, 16)
            for col, vec in ((b1c, b1), (gammac, gamma), (betac, beta)):
                sp.dma_start(col[:], vec).then_inc(consts_loaded, 16)
            sp.dma_start(b2b[:], b2.partition_broadcast(P)).then_inc(consts_loaded, 16)
            sp.dma_start(w2_stage[:], w2_v).then_inc(w2_loaded, 16)

            def next_adj(b):
                sp.wait_ge(dnh_ready, b)
                sp.wait_ge(adjt_done, b)
                load_adj(b)

            def step(b, adj_too, x_too):
                if adj_too:
                    next_adj(b + 2)
                if x_too:
                    sp.wait_ge(at_done, DT * b + DT)
                    sp.wait_ge(resid_ready, GB * b + GB)
                    sp.dma_start(x_sb[:], x_v[b + 1]).then_inc(x_loaded, 16)
                sp.wait_ge(norm_ready, b + 1)
                sp.dma_start(out_v[b], t_sb[:]).then_inc(stored, 16)

            next_adj(1)
            with sp.Fori(0, NB - 2) as b:
                step(b, True, True)
            step(NB - 2, False, True)
            step(NB - 1, False, False)
            sp.wait_ge(stored, 16 * NB)

        @block.tensor
        def _(pe):
            def transposes(src, dst, done):
                for g in range(GB):
                    last = pe.transpose(dst[:, g], src[:, g], ident[:])
                last.then_inc(done, 1)

            def prep_adjt(b):
                pe.wait_ge(adj_loaded, 16 * b + 16)
                transposes(adj_sb, prep4, adjt_done)

            def prep_dnht(b):
                pe.wait_ge(dnh_ready, b + 1)
                pe.wait_ge(ht_ready, b + 1)
                transposes(dnh, prep4, dnht_done)

            def prep_g(b):
                pe.wait_ge(beht_ready, b + 1)
                pe.wait_ge(dnht_ready, b + 1)
                for g in range(GB):
                    last = pe.matmul(prep4[:, g], beht[:, g], dnht[:, g], start=True, stop=True)
                last.then_inc(gt_done, 1)

            def aggregate_x(b, dt, first=False):
                if dt == 0:
                    pe.wait_ge(gt_ready, b + 1)
                    pe.wait_ge(x_loaded, 16 * b + 16)
                if not (first and dt < 2):
                    pe.wait_ge(atl_ready, DT * b + dt - 1)
                for g in range(GB):
                    last = pe.matmul(p_at[dt % 2][:, g * P:(g + 1) * P], x_sb[:, g, dt * P:(dt + 1) * P],
                                     gt[:, g], start=True, stop=True)
                last.then_inc(at_done, 1)

            def hidden(b, ht, first):
                if ht < MAIN:
                    if not first:
                        pe.wait_ge(ys_ready, GB * b)
                else:
                    pe.wait_ge(r_ready, HT * b + ht - MAIN + 1)
                acc = p_main[ht % MAIN]
                for dt in range(DT):
                    if ht == 0:
                        pe.wait_ge(ath_ready, DT * b + dt + 1)
                    cols = slice(ht * P, (ht + 1) * P)
                    pe.matmul(acc[:], w1h[:, dt, cols], ath[:, dt], start=dt == 0, stop=False)
                    pe.matmul(acc[:], w1l[:, dt, cols], ath[:, dt], start=False, stop=False)
                    if ht == 0:
                        pe.wait_ge(atl_ready, DT * b + dt + 1)
                    last = pe.matmul(acc[:], w1h[:, dt, cols], atl[:, dt], start=False, stop=dt == DT - 1)
                last.then_inc(z_done, 1)

            def project(b, g):
                step = HT + g
                if g < GB - 1:
                    pe.wait_ge(r_ready, HT * b + step - MAIN + 1)
                else:
                    pe.wait_ge(ys_ready, GB * b + 1)
                acc = p_main[step % MAIN]
                cols = slice(g * P, (g + 1) * P)
                for ht in range(HT):
                    if g == 0:
                        pe.wait_ge(rh_ready, HT * b + ht + 1)
                        pe.wait_ge(rl_ready, HT * b + ht + 1)
                    pe.matmul(acc[:], rh[:, ht, cols], w2h[:, ht], start=ht == 0, stop=False)
                    pe.matmul(acc[:], rh[:, ht, cols], w2l[:, ht], start=False, stop=False)
                    last = pe.matmul(acc[:], rl[:, ht, cols], w2h[:, ht], start=False, stop=ht == HT - 1)
                last.then_inc(y_done, 1)

            def statistics(b):
                pe.wait_ge(sum_steps, SUM_STEPS * (b + 1))
                for g in range(GB):
                    cols = slice(g * P, (g + 1) * P)
                    pe.matmul(stat4[:, g], sums[:, 0, cols], pick[:, 0], start=True, stop=False)
                    last = pe.matmul(stat4[:, g], sums[:, 1, cols], pick[:, 1], start=False, stop=True)
                last.then_inc(stats_done, 1)

            def aggregate_y(b, g, first):
                if not (first and g == 0):
                    pe.wait_ge(t_ready, GB * b + g)
                if g == 0:
                    pe.wait_ge(gth_ready, b + 1)
                    pe.wait_ge(gtl_ready, b + 1)
                pe.wait_ge(yh_ready, GB * b + g + 1)
                pe.matmul(p_agg[:], gth[:, g], yh[:, g % 2], start=True, stop=False)
                pe.matmul(p_agg[:], gtl[:, g], yh[:, g % 2], start=False, stop=False)
                pe.wait_ge(yl_ready, GB * b + g + 1)
                pe.matmul(p_agg[:], gth[:, g], yl[:, g % 2], start=False, stop=True).then_inc(agg_done, 1)

            pe.wait_ge(made, 2)
            prep_adjt(0)
            prep_dnht(0)
            prep_g(0)
            for dt in range(DT):
                aggregate_x(0, dt, True)

            pe.wait_ge(rep_ready, 2)
            pe.wait_ge(w2_loaded, 16)
            for ht in range(HT):
                pe.matmul(p_agg[:], gamma_rep[:, ht], w2_stage[:, ht], start=ht == 0, stop=ht == HT - 1)
                last = pe.matmul(p_stat[:], beta_rep[:, ht], w2_stage[:, ht], start=ht == 0, stop=ht == HT - 1)
            last.then_inc(w2sums_done, 1)
            pe.wait_ge(w1_ready, 1)

            def body(b, first, last_batch):
                for ht in range(HT):
                    hidden(b, ht, first)
                    if not last_batch:
                        if ht == 1:
                            prep_adjt(b + 1)
                        elif ht == 3:
                            prep_dnht(b + 1)
                        elif ht == 5:
                            prep_g(b + 1)
                if first:
                    pe.wait_ge(w2_ready, 1)
                project(b, 0)
                statistics(b)
                if not last_batch:
                    aggregate_x(b + 1, 0)
                project(b, 1)
                aggregate_y(b, 0, first)
                if not last_batch:
                    aggregate_x(b + 1, 1)
                project(b, 2)
                aggregate_y(b, 1, first)
                if not last_batch:
                    aggregate_x(b + 1, 2)
                project(b, 3)
                aggregate_y(b, 2, first)
                if not last_batch:
                    aggregate_x(b + 1, 3)
                aggregate_y(b, 3, first)

            batches(pe, body)

        @block.scalar
        def _(act):
            def copy_dnht(b):
                act.wait_ge(dnht_done, b + 1)
                act.activation(dnht[:], prep4, ACT.Copy).then_inc(dnht_ready, 1)

            def copy_gt(b):
                act.wait_ge(gt_done, b + 1)
                act.activation(gt[:], prep4, ACT.Copy).then_inc(gt_ready, 1)

            def split_at(b, dt):
                act.wait_ge(at_done, DT * b + dt + 1)
                act.activation(ath[:, dt], p_at[dt % 2][:], ACT.Copy).then_inc(ath_ready, 1)

            act.wait_ge(w1_loaded, 32)
            for i in range(2):
                act.activation(w1h[:, 2 * i:2 * i + 2], w1_stage[i], ACT.Copy).then_inc(w1h_ready, 1)
            copy_dnht(0)
            copy_gt(0)
            for dt in range(DT):
                split_at(0, dt)
            for ht in range(HT):
                act.wait_ge(w2c_ready, ht + 1)
                act.activation(w2h[:, ht], w2_stage[:, ht], ACT.Copy).then_inc(w2h_ready, 1)
            act.wait_ge(w2_ready, 1)
            act.wait_ge(consts_loaded, 64)

            def relu(b, ht, first):
                bias = b1c[:, ht:ht + 1]
                act.wait_ge(z_done, HT * b + ht + 1)
                act.activation(rh[:, ht], p_main[ht % MAIN][:], ACT.Relu, bias=bias).then_inc(rh_ready, 1)
                if not first:
                    act.wait_ge(rl_ready, HT * (b - 1) + ht + 1)
                    act.wait_ge(sum_steps, SUM_STEPS * b)
                act.activation(rr[:, ht], p_main[ht % MAIN][:], ACT.Relu, bias=bias).then_inc(r_ready, 1)
                if ht >= QS:
                    act.wait_ge(sum_steps, SUM_STEPS * b + 2 * max(ht - QS, 1))
                act.wait_ge(r_ready, HT * b + ht + 1)
                act.activation(rq[:, ht % QS], rr[:, ht], ACT.Square).then_inc(q_ready, 1)

            def body(b, first, last_batch):
                for ht in range(HT):
                    relu(b, ht, first)
                    if ht == 0:
                        act.wait_ge(gt_ready, b + 1)
                        act.activation(gth[:], gt[:], ACT.Copy).then_inc(gth_ready, 1)
                    if not last_batch:
                        if ht == 4:
                            copy_dnht(b + 1)
                        elif ht == 6:
                            act.wait_ge(gtl_ready, b + 1)
                            copy_gt(b + 1)
                for g in range(GB):
                    if not last_batch:
                        split_at(b + 1, g)
                    act.wait_ge(ys_ready, GB * b + g + 1)
                    act.activation(yh[:, g % 2], ys[:, g % 2], ACT.Copy).then_inc(yh_ready, 1)

            batches(act, body)

        @block.vector
        def _(dve):
            def guarded_reciprocal(s, n0, total, pos, safe, rec, res):
                dve.tensor_scalar(pos, total, 0.0, None, ALU.is_gt).then_inc(s, 1)
                dve.tensor_scalar(safe, total, TINY, None, ALU.max).then_inc(s, 1)
                dve.wait_ge(s, n0 + 2)
                dve.reciprocal(rec, safe).then_inc(s, 1)
                dve.wait_ge(s, n0 + 3)
                dve.tensor_tensor(res, rec, pos, ALU.mult).then_inc(s, 1)
                dve.wait_ge(s, n0 + 4)

            def prep_dn(b, first=False):
                n = DN_STEPS * b
                dve.wait_ge(adj_loaded, 16 * b + 16)
                dve.wait_ge(wrow_loaded, 16 * b + 16)
                dve.scalar_tensor_tensor(hw[:], adj_sb[:], 0.0, wrow[:], ALU.not_equal, ALU.mult).then_inc(dnorm, 1)
                dve.wait_ge(dnorm, n + 1)
                dve.tensor_reduce(dsum, hw[:], AX.X, ALU.add).then_inc(dnorm, 1)
                dve.wait_ge(dnorm, n + 2)
                guarded_reciprocal(dnorm, n + 2, dsum, dpos, dsafe, drec, dn)
                if not first:
                    dve.wait_ge(dnht_done, b)
                for g in range(GB):
                    last = dve.tensor_scalar(dnh[:, g], adj_sb[:, g], 0.0, dn[:, g:g + 1], ALU.not_equal, ALU.mult)
                last.then_inc(dnh_ready, 1)

            def prep_be(b, first=False):
                n = BE_STEPS * b
                dve.wait_ge(adjt_done, b + 1)
                dve.tensor_scalar(ht_sb[:], prep4, 0.0, None, ALU.not_equal).then_inc(ht_ready, 1)
                dve.wait_ge(ht_ready, b + 1)
                dve.tensor_reduce(deg, ht_sb[:], AX.X, ALU.add).then_inc(benorm, 1)
                dve.wait_ge(benorm, n + 1)
                guarded_reciprocal(benorm, n + 1, deg, bpos, bsafe, brec, be)
                if not first:
                    dve.wait_ge(gt_done, b)
                for g in range(GB):
                    last = dve.tensor_scalar(beht[:, g], ht_sb[:, g], be[:, g:g + 1], None, ALU.mult)
                last.then_inc(beht_ready, 1)

            def split_at(b, dt):
                dve.wait_ge(ath_ready, DT * b + dt + 1)
                dve.tensor_tensor(atl[:, dt], p_at[dt % 2][:], ath[:, dt].bitcast(F32), ALU.subtract)\
                   .then_inc(atl_ready, 1)

            dve.memset(ones[:], 1.0).then_inc(zeroed, 1)
            dve.memset(pick[:], 0.0).then_inc(zeroed, 1)
            dve.memset(neghalf[:], -0.5).then_inc(zeroed, 1)
            dve.wait_ge(zeroed, 3)
            for i in range(2):
                last = dve.memset(pick[:, i, 64 * i:64 * i + 64], 1.0)
            last.then_inc(made, 1)
            prep_dn(0, True)
            prep_be(0, True)
            dve.wait_ge(consts_loaded, 64)
            for rep, col, scale in ((gamma_rep, gammac, 1.0 / DH), (beta_rep, betac, 1.0)):
                for ht in range(HT):
                    last = dve.tensor_scalar(rep[:, ht], ones[:], col[:, ht:ht + 1], scale, ALU.mult, ALU.mult)
                last.then_inc(rep_ready, 1)
            for i in range(2):
                dve.wait_ge(w1h_ready, i + 1)
                last = dve.tensor_tensor(w1l[:, 2 * i:2 * i + 2], w1_stage[i], w1h[:, 2 * i:2 * i + 2].bitcast(F32),
                                         ALU.subtract)
            last.then_inc(w1_ready, 1)
            for dt in range(DT):
                split_at(0, dt)

            dve.wait_ge(w2sums_done, 1)
            dve.tensor_copy(wbb[:], p_stat[:])
            for ht in range(HT):
                dve.scalar_tensor_tensor(w2_stage[:, ht], w2_stage[:, ht], gammac[:, ht:ht + 1], p_agg[:],
                                         ALU.mult, ALU.subtract).then_inc(w2c_ready, 1)
            for ht in range(HT):
                dve.wait_ge(w2h_ready, ht + 1)
                last = dve.tensor_tensor(w2l[:, ht], w2_stage[:, ht], w2h[:, ht].bitcast(F32), ALU.subtract)
            last.then_inc(w2_ready, 1)

            def residual(b, g):
                if g == 0:
                    dve.wait_ge(x_loaded, 16 * b + 16)
                dve.scalar_tensor_tensor(resid[:, g], x_sb[:, g], 2.0, b2b[:], ALU.mult, ALU.add)\
                   .then_inc(resid_ready, 1)

            def first_norm(b):
                n = VAR1_STEPS * b
                dve.wait_ge(stats_done, b + 1)
                dve.tensor_scalar(mean1, stat4[:, :, 0], 1.0 / DH, None, ALU.mult).then_inc(var1_steps, 1)
                dve.tensor_scalar(var1, stat4[:, :, 64], 1.0 / DH, EPS, ALU.mult, ALU.add).then_inc(var1_steps, 1)
                dve.wait_ge(var1_steps, n + 2)
                dve.tensor_tensor(msq1, mean1, mean1, ALU.mult).then_inc(var1_steps, 1)
                dve.wait_ge(var1_steps, n + 3)
                dve.tensor_tensor(var1, var1, msq1, ALU.subtract).then_inc(var1_steps, 1)
                dve.wait_ge(var1_steps, n + 4)
                dve.tensor_scalar(var1, var1, EPS, None, ALU.max).then_inc(var1_steps, 1)

            def normalised(b, g):
                if g == 0:
                    dve.wait_ge(rstd1_ready, b + 1)
                dve.wait_ge(y_done, GB * b + g + 1)
                dve.scalar_tensor_tensor(ys[:, g % 2], p_main[(HT + g) % MAIN][:], rstd1[:, g:g + 1], wbb[:],
                                         ALU.mult, ALU.add).then_inc(ys_ready, 1)

            def split_y(b, g):
                dve.wait_ge(yh_ready, GB * b + g + 1)
                dve.tensor_tensor(yl[:, g % 2], ys[:, g % 2], yh[:, g % 2].bitcast(F32), ALU.subtract)\
                   .then_inc(yl_ready, 1)

            def add_residual(b, g, first):
                if g == 0 and not first:
                    dve.wait_ge(stored, 16 * b)
                dve.wait_ge(agg_done, GB * b + g + 1)
                dve.tensor_tensor(t_sb[:, g], p_agg[:], resid[:, g], ALU.add).then_inc(t_ready, 1)
                dve.wait_ge(t_ready, GB * b + g + 1)
                dve.bn_stats(bns[:, g], t_sb[:, g]).then_inc(bns_ready, 1)

            def last_norm(b):
                dve.wait_ge(bns_ready, GB * b + GB)
                n = VAR2_STEPS * b
                mean_even, m2_even, mean_odd, m2_odd = (bns[:, :, i] for i in (1, 2, 4, 5))
                dve.tensor_tensor(mean2, mean_even, mean_odd, ALU.add).then_inc(var2_steps, 1)
                dve.tensor_tensor(diff2, mean_even, mean_odd, ALU.subtract).then_inc(var2_steps, 1)
                dve.tensor_tensor(var2, m2_even, m2_odd, ALU.add).then_inc(var2_steps, 1)
                dve.wait_ge(var2_steps, n + 3)
                dve.tensor_scalar(mean2, mean2, 0.5, None, ALU.mult).then_inc(var2_steps, 1)
                dve.scalar_tensor_tensor(diff2, diff2, 0.25, diff2, ALU.mult, ALU.mult).then_inc(var2_steps, 1)
                dve.tensor_scalar(var2, var2, 1.0 / DI, EPS, ALU.mult, ALU.add).then_inc(var2_steps, 1)
                dve.wait_ge(var2_steps, n + 6)
                dve.tensor_tensor(var2, var2, diff2, ALU.add).then_inc(var2_steps, 1)
                dve.wait_ge(rstd2_ready, b + 1)
                for g in range(GB):
                    last = dve.tensor_scalar(t_sb[:, g], t_sb[:, g], mean2[:, g:g + 1], rstd2[:, g:g + 1],
                                             ALU.subtract, ALU.mult)
                last.then_inc(norm_ready, 1)

            def body(b, first, last_batch):
                for ht in range(HT):
                    dve.wait_ge(r_ready, HT * b + ht + 1)
                    dve.tensor_tensor(rl[:, ht], rr[:, ht], rh[:, ht].bitcast(F32), ALU.subtract)\
                       .then_inc(rl_ready, 1)
                    if ht == 0:
                        dve.wait_ge(gth_ready, b + 1)
                        dve.tensor_tensor(gtl[:], gt[:], gth[:].bitcast(F32), ALU.subtract).then_inc(gtl_ready, 1)
                    if ht < GB:
                        residual(b, ht)
                    if not last_batch:
                        if ht == 1:
                            prep_dn(b + 1)
                        elif ht == 2:
                            prep_be(b + 1)
                first_norm(b)
                for g in range(GB):
                    if g == 0 and not last_batch:
                        split_at(b + 1, g)
                    normalised(b, g)
                    if g > 0:
                        add_residual(b, g - 1, first)
                        if not last_batch:
                            split_at(b + 1, g)
                    split_y(b, g)
                add_residual(b, GB - 1, first)
                last_norm(b)

            batches(dve, body)

        @block.gpsimd
        def _(pool):
            pool.memset(ident[:], 0.0).then_inc(zeroed_ident, 1)
            pool.wait_ge(zeroed_ident, 1)
            pool.affine_select(out=ident[:], in_=ident[:], compare_op=ALU.not_equal, fill=1.0, base=0,
                               pattern=[[-1, P]], channel_multiplier=1).then_inc(made, 1)

            def body(b, first, last_batch):
                n = SUM_STEPS * b
                for ht in range(1, HT):
                    for i, (src, ready) in enumerate(((rr, r_ready), (rq, q_ready))):
                        slots = HT if i == 0 else QS
                        pool.wait_ge(ready, HT * b + ht + 1)
                        if ht == 1:
                            pool.tensor_tensor(sums[:, i], src[:, 0], src[:, 1], ALU.add).then_inc(sum_steps, 1)
                        else:
                            pool.wait_ge(sum_steps, n + 2 * (ht - 2) + i + 1)
                            pool.tensor_tensor(sums[:, i], sums[:, i], src[:, ht % slots], ALU.add)\
                                .then_inc(sum_steps, 1)
                pool.wait_ge(var1_steps, VAR1_STEPS * (b + 1))
                pool.tensor_tensor(rstd1, var1, neghalf[:], ALU.pow).then_inc(rstd1_ready, 1)
                pool.wait_ge(var2_steps, VAR2_STEPS * (b + 1))
                pool.tensor_tensor(rstd2, var2, neghalf[:], ALU.pow).then_inc(rstd2_ready, 1)

            batches(pool, body)


_INS = ["x", "adj", "w1t", "b1", "gamma", "beta", "w2t", "b2"]


def kernel(x, adj, L0_gnn_W1, L0_gnn_b1, L0_gnn_gamma, L0_gnn_beta, L0_gnn_W2, L0_gnn_b2):
    import numpy as np
    import concourse.bacc as bacc
    from concourse.bass_utils import run_bass_kernel_spmd

    def tiles(vector):
        return np.asarray(vector).reshape(-1, P).T

    given = dict(zip(_INS, (x, adj, np.asarray(L0_gnn_W1).T, tiles(L0_gnn_b1), tiles(L0_gnn_gamma),
                            tiles(L0_gnn_beta), np.asarray(L0_gnn_W2).T, L0_gnn_b2)))
    nc = bacc.Bacc("TRN2", target_bir_lowering=False, num_devices=1)
    arrays, args = {}, []
    for name, a in given.items():
        a = np.ascontiguousarray(a)
        arrays[name] = a
        args.append(nc.dram_tensor(name, a.shape, mybir.dt.from_np(a.dtype), kind="ExternalInput").ap())
    args.append(nc.dram_tensor("out", x.shape, F32, kind="ExternalOutput").ap())
    adj_resnorm_kernel(nc, *args)
    r = run_bass_kernel_spmd(nc, [arrays], core_ids=[0])
    return r.results[0]["out"]
```

```python
from contextlib import ExitStack

import concourse.bass as bass
from concourse import mybir

F32 = mybir.dt.float32
F32R = mybir.dt.float32r
ALU = mybir.AluOpType
ACT = mybir.ActivationFunctionType
AX = mybir.AxisListType

P = 128
GB = 4
COLS = GB * P
EPS = 1e-5
TINY = 1.2e-38


def adj_resnorm_kernel(nc, x, adj, w1t, b1, gamma, beta, w2t, b2, out):
    N, C, DI = x.shape
    DH = w1t.shape[1]
    assert C == P and N % GB == 0 and DI == COLS and w2t.shape == (DH, DI)
    NB = N // GB
    DT = DI // P
    HT = DH // P
    MAIN = 3
    assert (HT + GB) % MAIN == 0 and HT >= 8 and DT == 4 and GB == 4

    x_v = x.rearrange("(n g) c d -> n c g d", g=GB)
    adj_v = adj.rearrange("(n g) c e -> n c g e", g=GB)
    w_v = adj[:, 0, :].rearrange("(n g) e -> n g e", g=GB)
    out_v = out.rearrange("(n g) c d -> n c g d", g=GB)
    w1_v = w1t.rearrange("(t p) h -> p t h", p=P)
    w2_v = w2t.rearrange("(t p) d -> p t d", p=P)

    with ExitStack() as ctx:
        def sb(name, shape, dt=F32):
            return ctx.enter_context(nc.sbuf_tensor(name, shape, dt))

        def bank(name):
            return ctx.enter_context(nc.psum_tensor(name, [P, COLS], F32))

        def sem(name):
            return ctx.enter_context(nc.semaphore(name))

        w1h = sb("w1h", [P, DT, DH], F32R)
        w1l = sb("w1l", [P, DT, DH], F32R)
        w2h = sb("w2h", [P, HT, DI], F32R)
        w2l = sb("w2l", [P, HT, DI], F32R)
        ident = sb("ident", [P, P])
        ones = sb("ones", [P, P])
        b1c = sb("b1c", [P, HT])
        gammac = sb("gammac", [P, HT])
        betac = sb("betac", [P, HT])
        b2b = sb("b2b", [P, DI])
        wbb = sb("wbb", [P, DI])
        neghalf = sb("neghalf", [P, GB])
        adj_sb = sb("adj_sb", [P, GB, P])
        wrow = sb("wrow", [P, GB, P])
        x_sb = sb("x_sb", [P, GB, DI])
        hw = sb("hw", [P, GB, P])
        dnh = sb("dnh", [P, GB, P])
        ht_sb = sb("ht_sb", [P, GB, P])
        beht = sb("beht", [P, GB, P])
        dnht = sb("dnht", [P, GB, P])
        gt = sb("gt", [P, GB, P])
        gth = sb("gth", [P, GB, P], F32R)
        gtl = sb("gtl", [P, GB, P], F32R)
        small = sb("small", [P, 22, GB])
        ath = sb("ath", [P, DT, COLS], F32R)
        atl = sb("atl", [P, DT, COLS], F32R)
        RS = 4
        rr = sb("rr", [P, RS, COLS])
        rh = sb("rh", [P, HT, COLS], F32R)
        rl = sb("rl", [P, HT, COLS], F32R)
        rq = sb("rq", [P, RS, COLS])
        sums = sb("sums", [P, 2, COLS])
        ys = sb("ys", [P, 2, DI])
        yh = sb("yh", [P, 2, DI], F32R)
        yl = sb("yl", [P, 2, DI], F32R)
        resid = sb("resid", [P, GB, DI])
        t_sb = sb("t_sb", [P, GB, DI])
        bns = sb("bns", [P, GB, 6])

        p_main = [bank(f"p_main{i}") for i in range(MAIN)]
        p_at = [bank(f"p_at{i}") for i in range(2)]
        p_prep, p_agg, p_stat = bank("p_prep"), bank("p_agg"), bank("p_stat")
        prep4 = p_prep[:].rearrange("p (g c) -> p g c", g=GB)
        stat4 = p_stat[:].rearrange("p (g c) -> p g c", g=GB)
        sums4 = sums[:].rearrange("p i (g c) -> p i g c", g=GB)

        dsum, dpos, dsafe, drec, dn = (small[:, i] for i in range(5))
        deg, bpos, bsafe, brec, be = (small[:, i] for i in range(5, 10))
        mean1, msq1, var1, rstd1, mean2, diff2, var2, rstd2, sum1, sumsq1, negmean2, bias2 = (
            small[:, i] for i in range(10, 22))

        w1_stage = [resid[:].rearrange("p g d -> p (g d)").rearrange("p (t h) -> p t h", h=DH),
                    t_sb[:].rearrange("p g d -> p (g d)").rearrange("p (t h) -> p t h", h=DH)]
        w2_spare = sb("w2_spare", [P, HT // 2, DI])
        w2_stage = [w2_spare[:, i] for i in range(HT // 2)] + [t_sb[:, i] for i in range(HT // 2)]
        beta_sum = wbb[:]
        gamma_rep = ys[:].rearrange("p a d -> p (a d)").rearrange("p (t c) -> p t c", c=P)

        consts_loaded, w1_loaded, w2_loaded = sem("consts_loaded"), [sem("w1_loaded0"), sem("w1_loaded1")], [sem("w2_loaded0"), sem("w2_loaded1")]
        adj_loaded, wrow_loaded, x_loaded, stored = sem("adj_loaded"), sem("wrow_loaded"), sem("x_loaded"), sem("stored")
        constants, ident_zeroed, ident_ready = sem("constants"), sem("ident_zeroed"), sem("ident_ready")
        w1h_ready, w1_ready = sem("w1h_ready"), sem("w1_ready")
        rep_ready, w2mean_done, w2beta_done, wb_ready, beta_steps, w2c_ready, w2h_ready = (
            sem(n) for n in ("rep_ready", "w2mean_done", "w2beta_done", "wb_ready", "beta_steps", "w2c_ready", "w2h_ready"))
        adjt_done, dnht_done, gt_done, at_done = sem("adjt_done"), sem("dnht_done"), sem("gt_done"), sem("at_done")
        z_done, y_done, stats_done, statsq_done, agg_done = (
            sem(n) for n in ("z_done", "y_done", "stats_done", "statsq_done", "agg_done"))
        rh_ready, r_ready, q_ready, norm_ready = sem("rh_ready"), sem("r_ready"), sem("q_ready"), sem("norm_ready")
        dnht_ready, gt_ready, gth_ready, ath_ready, yh_ready = (
            sem(n) for n in ("dnht_ready", "gt_ready", "gth_ready", "ath_ready", "yh_ready"))
        dnorm, dnh_ready, ht_ready, benorm, beht_ready = (
            sem(n) for n in ("dnorm", "dnh_ready", "ht_ready", "benorm", "beht_ready"))
        gtl_ready, atl_ready, rl_ready, sum_steps, resid_ready = (
            sem(n) for n in ("gtl_ready", "atl_ready", "rl_ready", "sum_steps", "resid_ready"))
        var1_steps, ys_ready, yl_ready, t_ready, bns_ready, var2_steps = (
            sem(n) for n in ("var1_steps", "ys_ready", "yl_ready", "t_ready", "bns_ready", "var2_steps"))
        sumsq_steps, rstd1_ready, rstd2_ready, bias2_ready, w2l_ready = (
            sem(n) for n in ("sumsq_steps", "rstd1_ready", "rstd2_ready", "bias2_ready", "w2l_ready"))

        block = ctx.enter_context(nc.Block())

        DN_STEPS, BE_STEPS, VAR1_STEPS, VAR2_STEPS = 6, 5, 7, 7
        SUM_STEPS = HT - 1

        def summed(b, ht):
            return SUM_STEPS * b + (ht + 1 if ht < 0 else max(ht, 1))

        def batches(eng, body):
            body(0, True, False)
            with nc.Fori(1, NB - 1, engines=[eng.engine], hint_back_edge=True) as b:
                body(b, False, False)
            body(NB - 1, False, True)

        @block.sync
        def _(sp):
            def load_adj(b):
                sp.dma_start(adj_sb[:], adj_v[b]).then_inc(adj_loaded, 16)
                sp.dma_start(wrow[:], w_v[b].partition_broadcast(P)).then_inc(wrow_loaded, 16)

            load_adj(0)
            for i in range(2):
                sp.dma_start(w1_stage[i], w1_v[:, 2 * i:2 * i + 2]).then_inc(w1_loaded[i], 16)
            sp.dma_start(x_sb[:], x_v[0]).then_inc(x_loaded, 16)
            for col, vec in ((b1c, b1), (gammac, gamma), (betac, beta)):
                sp.dma_start(col[:], vec).then_inc(consts_loaded, 16)
            sp.dma_start(b2b[:], b2.partition_broadcast(P)).then_inc(consts_loaded, 16)
            sp.dma_start(w2_spare[:], w2_v[:, :HT // 2]).then_inc(w2_loaded[0], 16)

            def next_adj(b):
                sp.wait_ge(dnh_ready, b)
                sp.wait_ge(adjt_done, b)
                load_adj(b)

            def next_x(b):
                sp.wait_ge(at_done, DT * b)
                sp.wait_ge(resid_ready, GB * b)
                sp.dma_start(x_sb[:], x_v[b]).then_inc(x_loaded, 16)

            def store(b):
                sp.wait_ge(norm_ready, GB * b + GB)
                sp.dma_start(out_v[b], t_sb[:]).then_inc(stored, 16)

            next_adj(1)
            sp.wait_ge(w1_ready, 1)
            sp.dma_start(t_sb[:], w2_v[:, HT // 2:]).then_inc(w2_loaded[1], 16)
            next_adj(2)
            next_x(1)
            with nc.Fori(1, NB - 2, engines=[sp.engine], hint_back_edge=True) as b:
                next_adj(b + 2)
                next_x(b + 1)
                store(b - 1)
            next_x(NB - 1)
            for b in range(NB - 3, NB):
                store(b)
            sp.wait_ge(stored, 16 * NB)

        @block.tensor
        def _(pe):
            def transposes(src, dst, done):
                for g in range(GB):
                    last = pe.transpose(dst[:, g], src[:, g], ident[:])
                last.then_inc(done, 1)

            def prep_dnht(b, first=False):
                pe.wait_ge(dnh_ready, b + 1)
                if not first:
                    pe.wait_ge(var1_steps, VAR1_STEPS * (b - 1))
                transposes(dnh, prep4, dnht_done)

            def prep_adjt(b):
                pe.wait_ge(adj_loaded, 16 * b + 16)
                pe.wait_ge(dnht_ready, b + 1)
                transposes(adj_sb, prep4, adjt_done)

            def prep_g(b):
                pe.wait_ge(beht_ready, b + 1)
                pe.wait_ge(dnht_ready, b + 1)
                for g in range(GB):
                    last = pe.matmul(prep4[:, g], beht[:, g], dnht[:, g], start=True, stop=True)
                last.then_inc(gt_done, 1)

            def aggregate_x(b, dt, first=False):
                if dt == 0:
                    pe.wait_ge(gt_ready, b + 1)
                    pe.wait_ge(x_loaded, 16 * b + 16)
                if not (first and dt < 2):
                    pe.wait_ge(atl_ready, DT * b + dt - 1)
                for g in range(GB):
                    last = pe.matmul(p_at[dt % 2][:, g * P:(g + 1) * P], x_sb[:, g, dt * P:(dt + 1) * P],
                                     gt[:, g], start=True, stop=True)
                last.then_inc(at_done, 1)

            def hidden(b, ht, first):
                if ht < MAIN:
                    if not first:
                        pe.wait_ge(ys_ready, GB * b)
                else:
                    pe.wait_ge(r_ready, HT * b + ht - MAIN + 1)
                acc = p_main[ht % MAIN]
                for dt in range(DT):
                    if ht == 0:
                        pe.wait_ge(ath_ready, DT * b + dt + 1)
                    cols = slice(ht * P, (ht + 1) * P)
                    pe.matmul(acc[:], w1h[:, dt, cols], ath[:, dt], start=dt == 0, stop=False)
                    pe.matmul(acc[:], w1l[:, dt, cols], ath[:, dt], start=False, stop=False)
                    if ht == 0:
                        pe.wait_ge(atl_ready, DT * b + dt + 1)
                    last = pe.matmul(acc[:], w1h[:, dt, cols], atl[:, dt], start=False, stop=dt == DT - 1)
                last.then_inc(z_done, 1)

            def project(b, g):
                step = HT + g
                if g < GB - 1:
                    pe.wait_ge(r_ready, HT * b + step - MAIN + 1)
                else:
                    pe.wait_ge(ys_ready, GB * b + 1)
                acc = p_main[step % MAIN]
                cols = slice(g * P, (g + 1) * P)
                for ht in range(HT):
                    if g == 0:
                        pe.wait_ge(rh_ready, HT * b + ht + 1)
                        pe.wait_ge(rl_ready, HT * b + ht + 1)
                    pe.matmul(acc[:], rh[:, ht, cols], w2h[:, ht], start=ht == 0, stop=False)
                    pe.matmul(acc[:], rh[:, ht, cols], w2l[:, ht], start=False, stop=False)
                    last = pe.matmul(acc[:], rl[:, ht, cols], w2h[:, ht], start=False, stop=ht == HT - 1)
                last.then_inc(y_done, 1)

            def statistics(b, last_batch):
                pe.wait_ge(sum_steps, SUM_STEPS * (b + 1))
                transposes(sums4[:, 0], stat4, stats_done)
                if not last_batch:
                    pe.wait_ge(gt_ready, b + 2)
                pe.wait_ge(sumsq_steps, SUM_STEPS * (b + 1))
                transposes(sums4[:, 1], prep4, statsq_done)

            def aggregate_y(b, g, first):
                if not (first and g == 0):
                    pe.wait_ge(t_ready, GB * b + g)
                if g == 0:
                    pe.wait_ge(gtl_ready, b + 1)
                pe.wait_ge(yh_ready, GB * b + g + 1)
                pe.matmul(p_agg[:], gth[:, g], yh[:, g % 2], start=True, stop=False)
                pe.matmul(p_agg[:], gtl[:, g], yh[:, g % 2], start=False, stop=False)
                pe.wait_ge(yl_ready, GB * b + g + 1)
                pe.matmul(p_agg[:], gth[:, g], yl[:, g % 2], start=False, stop=True).then_inc(agg_done, 1)

            pe.wait_ge(ident_ready, 1)
            pe.wait_ge(adj_loaded, 16)
            transposes(adj_sb, stat4, adjt_done)
            prep_dnht(0, True)
            prep_g(0)
            for dt in range(DT):
                aggregate_x(0, dt, True)

            pe.wait_ge(w1_ready, 1)

            def weight_mean():
                pe.wait_ge(rep_ready, 1)
                for ht in range(HT):
                    pe.wait_ge(w2_loaded[ht // (HT // 2)], 16)
                    last = pe.matmul(p_agg[:], gamma_rep[:, ht], w2_stage[ht], start=ht == 0, stop=ht == HT - 1)
                last.then_inc(w2mean_done, 1)

            def weight_beta():
                pe.wait_ge(beta_steps, HT)
                pe.matmul(p_stat[:], ones[:], beta_sum, start=True, stop=True).then_inc(w2beta_done, 1)

            def body(b, first, last_batch):
                for ht in range(HT):
                    hidden(b, ht, first)
                    if ht == 0:
                        if first:
                            weight_mean()
                        else:
                            aggregate_y(b - 1, GB - 1, False)
                    if ht == 2 and first:
                        weight_beta()
                    if not last_batch:
                        if ht == 2:
                            prep_dnht(b + 1, first)
                        elif ht == 4:
                            prep_adjt(b + 1)
                        elif ht == 7:
                            prep_g(b + 1)
                for g in range(GB):
                    if g == 0 and first:
                        pe.wait_ge(w2l_ready, 1)
                    project(b, g)
                    if g == 0 and first:
                        pe.wait_ge(wb_ready, 1)
                    if g == 0:
                        statistics(b, last_batch)
                    if not last_batch:
                        aggregate_x(b + 1, g)
                    if g > 0:
                        aggregate_y(b, g - 1, first)
                if last_batch:
                    aggregate_y(b, GB - 1, False)

            batches(pe, body)

        @block.scalar
        def _(act):
            def copy_dnht(b):
                act.wait_ge(dnht_done, b + 1)
                act.activation(dnht[:], prep4, ACT.Copy).then_inc(dnht_ready, 1)

            def copy_gt(b):
                act.wait_ge(gt_done, b + 1)
                act.activation(gt[:], prep4, ACT.Copy).then_inc(gt_ready, 1)

            def split_at(b, dt):
                act.wait_ge(at_done, DT * b + dt + 1)
                act.activation(ath[:, dt], p_at[dt % 2][:], ACT.Copy).then_inc(ath_ready, 1)

            def split_w1(i):
                act.wait_ge(w1_loaded[i], 16)
                act.activation(w1h[:, 2 * i:2 * i + 2], w1_stage[i], ACT.Copy).then_inc(w1h_ready, 1)

            def split_w2(ht):
                act.wait_ge(w2c_ready, ht + 1)
                act.activation(w2h[:, ht], w2_stage[ht], ACT.Copy).then_inc(w2h_ready, 1)

            def apply_last_norm(b, g):
                act.activation(t_sb[:, g], t_sb[:, g], ACT.Identity, bias=bias2[:, g:g + 1],
                               scale=rstd2[:, g:g + 1]).then_inc(norm_ready, 1)

            split_w1(0)
            copy_dnht(0)
            split_w1(1)
            copy_gt(0)
            for dt in range(DT):
                split_at(0, dt)
            act.wait_ge(consts_loaded, 64)

            def relu(b, ht, first):
                bias = b1c[:, ht:ht + 1]
                act.wait_ge(z_done, HT * b + ht + 1)
                act.activation(rh[:, ht], p_main[ht % MAIN][:], ACT.Relu, bias=bias).then_inc(rh_ready, 1)
                if not (first and ht < RS):
                    act.wait_ge(rl_ready, HT * b + ht - RS + 1)
                    act.wait_ge(sum_steps, summed(b, ht - RS))
                act.activation(rr[:, ht % RS], p_main[ht % MAIN][:], ACT.Relu, bias=bias).then_inc(r_ready, 1)
                if not (first and ht < RS):
                    act.wait_ge(sumsq_steps, summed(b, ht - RS))
                act.wait_ge(r_ready, HT * b + ht + 1)
                act.activation(rq[:, ht % RS], rr[:, ht % RS], ACT.Square).then_inc(q_ready, 1)

            def body(b, first, last_batch):
                for ht in range(HT):
                    if ht == 3 and not last_batch:
                        copy_dnht(b + 1)
                    relu(b, ht, first)
                    if ht == 1:
                        act.wait_ge(gt_ready, b + 1)
                        if not first:
                            act.wait_ge(agg_done, GB * b)
                        act.activation(gth[:], gt[:], ACT.Copy).then_inc(gth_ready, 1)
                    if first and 2 <= ht < 2 + HT // 2:
                        split_w2(2 * ht - 4)
                        split_w2(2 * ht - 3)
                    if ht == 2 and not first:
                        act.wait_ge(bias2_ready, b)
                    if 2 <= ht < 2 + GB and not first:
                        apply_last_norm(b - 1, ht - 2)
                    if not last_batch:
                        if ht == 7:
                            act.wait_ge(gtl_ready, b + 1)
                            copy_gt(b + 1)
                for g in range(GB):
                    if not last_batch:
                        split_at(b + 1, g)
                    act.wait_ge(ys_ready, GB * b + g + 1)
                    act.activation(yh[:, g % 2], ys[:, g % 2], ACT.Copy).then_inc(yh_ready, 1)
                if last_batch:
                    act.wait_ge(bias2_ready, b + 1)
                    for g in range(GB):
                        apply_last_norm(b, g)

            batches(act, body)

        @block.vector
        def _(dve):
            def guarded_reciprocal(s, n0, total, pos, safe, rec, res):
                dve.tensor_scalar(pos, total, 0.0, None, ALU.is_gt).then_inc(s, 1)
                dve.tensor_scalar(safe, total, TINY, None, ALU.max).then_inc(s, 1)
                dve.wait_ge(s, n0 + 2)
                dve.reciprocal(rec, safe).then_inc(s, 1)
                dve.wait_ge(s, n0 + 3)
                dve.tensor_tensor(res, rec, pos, ALU.mult).then_inc(s, 1)
                dve.wait_ge(s, n0 + 4)

            def prep_dn(b, first=False):
                n = DN_STEPS * b
                dve.wait_ge(adj_loaded, 16 * b + 16)
                dve.wait_ge(wrow_loaded, 16 * b + 16)
                dve.scalar_tensor_tensor(hw[:], adj_sb[:], 0.0, wrow[:], ALU.not_equal, ALU.mult).then_inc(dnorm, 1)
                dve.wait_ge(dnorm, n + 1)
                dve.tensor_reduce(dsum, hw[:], AX.X, ALU.add).then_inc(dnorm, 1)
                dve.wait_ge(dnorm, n + 2)
                guarded_reciprocal(dnorm, n + 2, dsum, dpos, dsafe, drec, dn)
                if not first:
                    dve.wait_ge(dnht_done, b)
                for g in range(GB):
                    last = dve.tensor_scalar(dnh[:, g], adj_sb[:, g], 0.0, dn[:, g:g + 1], ALU.not_equal, ALU.mult)
                last.then_inc(dnh_ready, 1)

            def prep_be(b, first=False, source=prep4):
                n = BE_STEPS * b
                dve.wait_ge(adjt_done, b + 1)
                dve.tensor_scalar(ht_sb[:], source, 0.0, None, ALU.not_equal).then_inc(ht_ready, 1)
                dve.wait_ge(ht_ready, b + 1)
                dve.tensor_reduce(deg, ht_sb[:], AX.X, ALU.add).then_inc(benorm, 1)
                dve.wait_ge(benorm, n + 1)
                guarded_reciprocal(benorm, n + 1, deg, bpos, bsafe, brec, be)
                if not first:
                    dve.wait_ge(gt_done, b)
                for g in range(GB):
                    last = dve.tensor_scalar(beht[:, g], ht_sb[:, g], be[:, g:g + 1], None, ALU.mult)
                last.then_inc(beht_ready, 1)

            def split_at(b, dt):
                dve.wait_ge(ath_ready, DT * b + dt + 1)
                dve.tensor_tensor(atl[:, dt], p_at[dt % 2][:], ath[:, dt].bitcast(F32), ALU.subtract)\
                   .then_inc(atl_ready, 1)

            dve.memset(ones[:], 1.0).then_inc(constants, 1)
            dve.memset(neghalf[:], -0.5).then_inc(constants, 1)
            prep_dn(0, True)
            prep_be(0, True, stat4)
            for i in range(2):
                dve.wait_ge(w1h_ready, i + 1)
                last = dve.tensor_tensor(w1l[:, 2 * i:2 * i + 2], w1_stage[i], w1h[:, 2 * i:2 * i + 2].bitcast(F32),
                                         ALU.subtract)
            last.then_inc(w1_ready, 1)
            for dt in range(DT):
                split_at(0, dt)
            dve.wait_ge(constants, 1)
            dve.wait_ge(consts_loaded, 64)
            for ht in range(HT):
                last = dve.tensor_scalar(gamma_rep[:, ht], ones[:], gammac[:, ht:ht + 1], 1.0 / DH, ALU.mult, ALU.mult)
            last.then_inc(rep_ready, 1)

            def centre_w2():
                for ht in range(HT):
                    dve.wait_ge(w2_loaded[ht // (HT // 2)], 16)
                    if ht == 0:
                        dve.tensor_scalar(beta_sum, w2_stage[ht], betac[:, ht:ht + 1], None, ALU.mult)\
                           .then_inc(beta_steps, 1)
                    else:
                        dve.wait_ge(beta_steps, ht)
                        dve.scalar_tensor_tensor(beta_sum, w2_stage[ht], betac[:, ht:ht + 1], beta_sum,
                                                 ALU.mult, ALU.add).then_inc(beta_steps, 1)
                dve.wait_ge(w2mean_done, 1)
                for ht in range(HT):
                    dve.scalar_tensor_tensor(w2_stage[ht], w2_stage[ht], gammac[:, ht:ht + 1], p_agg[:],
                                             ALU.mult, ALU.subtract).then_inc(w2c_ready, 1)

            def residual(b, g):
                dve.wait_ge(x_loaded, 16 * b + 16)
                dve.scalar_tensor_tensor(resid[:, g], x_sb[:, g], 2.0, b2b[:], ALU.mult, ALU.add)\
                   .then_inc(resid_ready, 1)

            def first_norm(b):
                n = VAR1_STEPS * b
                dve.wait_ge(stats_done, b + 1)
                dve.tensor_reduce(sum1, stat4, AX.X, ALU.add).then_inc(var1_steps, 1)
                dve.wait_ge(var1_steps, n + 1)
                dve.tensor_scalar(mean1, sum1, 1.0 / DH, None, ALU.mult).then_inc(var1_steps, 1)
                dve.wait_ge(var1_steps, n + 2)
                dve.tensor_tensor(msq1, mean1, mean1, ALU.mult).then_inc(var1_steps, 1)
                dve.wait_ge(statsq_done, b + 1)
                dve.tensor_reduce(sumsq1, prep4, AX.X, ALU.add).then_inc(var1_steps, 1)
                dve.wait_ge(var1_steps, n + 4)
                dve.tensor_scalar(var1, sumsq1, 1.0 / DH, EPS, ALU.mult, ALU.add).then_inc(var1_steps, 1)
                dve.wait_ge(var1_steps, n + 5)
                dve.tensor_tensor(var1, var1, msq1, ALU.subtract).then_inc(var1_steps, 1)
                dve.wait_ge(var1_steps, n + 6)
                dve.tensor_scalar(var1, var1, EPS, None, ALU.max).then_inc(var1_steps, 1)

            def normalised(b, g):
                if g == 0:
                    dve.wait_ge(rstd1_ready, b + 1)
                dve.wait_ge(y_done, GB * b + g + 1)
                dve.scalar_tensor_tensor(ys[:, g % 2], p_main[(HT + g) % MAIN][:], rstd1[:, g:g + 1], wbb[:],
                                         ALU.mult, ALU.add).then_inc(ys_ready, 1)

            def split_y(b, g):
                dve.wait_ge(yh_ready, GB * b + g + 1)
                dve.tensor_tensor(yl[:, g % 2], ys[:, g % 2], yh[:, g % 2].bitcast(F32), ALU.subtract)\
                   .then_inc(yl_ready, 1)

            def add_residual(b, g, first):
                if g == 0 and not first:
                    dve.wait_ge(stored, 16 * b)
                dve.wait_ge(agg_done, GB * b + g + 1)
                dve.tensor_tensor(t_sb[:, g], p_agg[:], resid[:, g], ALU.add).then_inc(t_ready, 1)
                dve.wait_ge(t_ready, GB * b + g + 1)
                dve.bn_stats(bns[:, g], t_sb[:, g]).then_inc(bns_ready, 1)

            def last_norm(b):
                dve.wait_ge(bns_ready, GB * b + GB)
                n = VAR2_STEPS * b
                mean_even, m2_even, mean_odd, m2_odd = (bns[:, :, i] for i in (1, 2, 4, 5))
                dve.tensor_tensor(mean2, mean_even, mean_odd, ALU.add).then_inc(var2_steps, 1)
                dve.tensor_tensor(diff2, mean_even, mean_odd, ALU.subtract).then_inc(var2_steps, 1)
                dve.tensor_tensor(var2, m2_even, m2_odd, ALU.add).then_inc(var2_steps, 1)
                dve.wait_ge(var2_steps, n + 3)
                dve.tensor_scalar(negmean2, mean2, -0.5, None, ALU.mult).then_inc(var2_steps, 1)
                dve.scalar_tensor_tensor(diff2, diff2, 0.25, diff2, ALU.mult, ALU.mult).then_inc(var2_steps, 1)
                dve.tensor_scalar(var2, var2, 1.0 / DI, EPS, ALU.mult, ALU.add).then_inc(var2_steps, 1)
                dve.wait_ge(var2_steps, n + 6)
                dve.tensor_tensor(var2, var2, diff2, ALU.add).then_inc(var2_steps, 1)

            def add_tile(b, ht):
                if ht == 1:
                    dve.tensor_tensor(sums[:, 0], rr[:, 0], rr[:, 1], ALU.add).then_inc(sum_steps, 1)
                elif ht > 1:
                    dve.wait_ge(sum_steps, SUM_STEPS * b + ht - 1)
                    dve.tensor_tensor(sums[:, 0], sums[:, 0], rr[:, ht % RS], ALU.add).then_inc(sum_steps, 1)

            def body(b, first, last_batch):
                if not last_batch:
                    prep_dn(b + 1)
                if first:
                    centre_w2()
                for ht in range(HT):
                    dve.wait_ge(r_ready, HT * b + ht + 1)
                    dve.tensor_tensor(rl[:, ht], rr[:, ht % RS], rh[:, ht].bitcast(F32), ALU.subtract)\
                       .then_inc(rl_ready, 1)
                    if ht == 0 and not first:
                        add_residual(b - 1, GB - 1, False)
                        last_norm(b - 1)
                        residual(b, GB - 1)
                    add_tile(b, ht)
                    if ht < GB and first:
                        residual(b, ht)
                    if ht == 4 and not last_batch:
                        prep_be(b + 1)
                    if ht == 5 and first:
                        dve.wait_ge(w2beta_done, 1)
                        dve.tensor_copy(wbb[:], p_stat[:]).then_inc(wb_ready, 1)
                first_norm(b)
                if first:
                    dve.wait_ge(wb_ready, 1)
                for g in range(GB):
                    if g == 0 and not last_batch:
                        split_at(b + 1, g)
                    normalised(b, g)
                    if g > 0:
                        if not last_batch:
                            split_at(b + 1, g)
                        add_residual(b, g - 1, first)
                    split_y(b, g)
                    if not last_batch:
                        if g > 0:
                            residual(b + 1, g - 1)
                if last_batch:
                    add_residual(b, GB - 1, False)
                    last_norm(b)

            batches(dve, body)

        @block.gpsimd
        def _(pool):
            pool.memset(ident[:], 0.0).then_inc(ident_zeroed, 1)
            pool.wait_ge(ident_zeroed, 1)
            pool.affine_select(out=ident[:], in_=ident[:], compare_op=ALU.not_equal, fill=1.0, base=0,
                               pattern=[[-1, P]], channel_multiplier=1).then_inc(ident_ready, 1)

            def root2(b):
                pool.wait_ge(var2_steps, VAR2_STEPS * (b + 1))
                pool.tensor_tensor(rstd2, var2, neghalf[:], ALU.pow).then_inc(rstd2_ready, 1)
                pool.wait_ge(rstd2_ready, b + 1)
                pool.tensor_tensor(bias2, negmean2, rstd2, ALU.mult).then_inc(bias2_ready, 1)

            def split_w2(ht):
                pool.wait_ge(w2h_ready, ht + 1)
                low = pool.tensor_tensor(w2l[:, ht], w2_stage[ht], w2h[:, ht].bitcast(F32), ALU.subtract)
                if ht == HT - 1:
                    low.then_inc(w2l_ready, 1)

            def body(b, first, last_batch):
                if not first:
                    root2(b - 1)
                pool.wait_ge(gth_ready, b + 1)
                pool.tensor_tensor(gtl[:], gt[:], gth[:].bitcast(F32), ALU.subtract).then_inc(gtl_ready, 1)
                for ht in range(1, HT):
                    pool.wait_ge(q_ready, HT * b + ht + 1)
                    if ht == 1:
                        pool.tensor_tensor(sums[:, 1], rq[:, 0], rq[:, 1], ALU.add).then_inc(sumsq_steps, 1)
                    else:
                        pool.wait_ge(sumsq_steps, SUM_STEPS * b + ht - 1)
                        pool.tensor_tensor(sums[:, 1], sums[:, 1], rq[:, ht % RS], ALU.add).then_inc(sumsq_steps, 1)
                    if first and 2 <= ht < 2 + HT // 2:
                        split_w2(2 * ht - 4)
                        split_w2(2 * ht - 3)
                pool.wait_ge(var1_steps, VAR1_STEPS * (b + 1))
                pool.tensor_tensor(rstd1, var1, neghalf[:], ALU.pow).then_inc(rstd1_ready, 1)
                if last_batch:
                    root2(b)

            batches(pool, body)


_INS = ["x", "adj", "w1t", "b1", "gamma", "beta", "w2t", "b2"]


def kernel(x, adj, L0_gnn_W1, L0_gnn_b1, L0_gnn_gamma, L0_gnn_beta, L0_gnn_W2, L0_gnn_b2):
    import numpy as np
    import concourse.bacc as bacc
    from concourse.bass_utils import run_bass_kernel_spmd

    def tiles(vector):
        return np.asarray(vector).reshape(-1, P).T

    given = dict(zip(_INS, (x, adj, np.asarray(L0_gnn_W1).T, tiles(L0_gnn_b1), tiles(L0_gnn_gamma),
                            tiles(L0_gnn_beta), np.asarray(L0_gnn_W2).T, L0_gnn_b2)))
    nc = bacc.Bacc("TRN2", target_bir_lowering=False, num_devices=1)
    arrays, args = {}, []
    for name, a in given.items():
        a = np.ascontiguousarray(a)
        arrays[name] = a
        args.append(nc.dram_tensor(name, a.shape, mybir.dt.from_np(a.dtype), kind="ExternalInput").ap())
    args.append(nc.dram_tensor("out", x.shape, F32, kind="ExternalOutput").ap())
    adj_resnorm_kernel(nc, *args)
    r = run_bass_kernel_spmd(nc, [arrays], core_ids=[0])
    return r.results[0]["out"]
```

```python
from contextlib import ExitStack

import concourse.bass as bass
from concourse import mybir

F32 = mybir.dt.float32
F32R = mybir.dt.float32r
ALU = mybir.AluOpType
ACT = mybir.ActivationFunctionType
AX = mybir.AxisListType

P = 128
GB = 4
COLS = GB * P
EPS = 1e-5
TINY = 1.2e-38


def adj_resnorm_kernel(nc, x, adj, w1t, b1, gamma, beta, w2t, b2, out):
    N, C, DI = x.shape
    DH = w1t.shape[1]
    assert C == P and N % GB == 0 and DI == COLS and w2t.shape == (DH, DI)
    NB = N // GB
    DT = DI // P
    HT = DH // P
    MAIN = 3
    assert (HT + GB) % MAIN == 0 and HT >= 8 and DT == 4 and GB == 4

    x_v = x.rearrange("(n g) c d -> n c g d", g=GB)
    adj_v = adj.rearrange("(n g) c e -> n c g e", g=GB)
    w_v = adj[:, 0, :].rearrange("(n g) e -> n g e", g=GB)
    out_v = out.rearrange("(n g) c d -> n c g d", g=GB)
    w1_v = w1t.rearrange("(t p) h -> p t h", p=P)
    w2_v = w2t.rearrange("(t p) d -> p t d", p=P)

    with ExitStack() as ctx:
        def sb(name, shape, dt=F32):
            return ctx.enter_context(nc.sbuf_tensor(name, shape, dt))

        def bank(name):
            return ctx.enter_context(nc.psum_tensor(name, [P, COLS], F32))

        def sem(name):
            return ctx.enter_context(nc.semaphore(name))

        w1h = sb("w1h", [P, DT, DH], F32R)
        w1l = sb("w1l", [P, DT, DH], F32R)
        w2h = sb("w2h", [P, HT, DI], F32R)
        w2l = sb("w2l", [P, HT, DI], F32R)
        ident = sb("ident", [P, P])
        ones = sb("ones", [P, P])
        b1c = sb("b1c", [P, HT])
        gammac = sb("gammac", [P, HT])
        betac = sb("betac", [P, HT])
        b2b = sb("b2b", [P, DI])
        wbb = sb("wbb", [P, DI])
        neghalf = sb("neghalf", [P, GB])
        adj_sb = sb("adj_sb", [P, GB, P])
        wrow = sb("wrow", [P, GB, P])
        x_sb = sb("x_sb", [P, GB, DI])
        hw = sb("hw", [P, GB, P])
        dnh = sb("dnh", [P, GB, P])
        ht_sb = sb("ht_sb", [P, GB, P])
        beht = sb("beht", [P, GB, P])
        dnht = sb("dnht", [P, GB, P])
        gt = sb("gt", [P, GB, P])
        gth = sb("gth", [P, GB, P], F32R)
        gtl = sb("gtl", [P, GB, P], F32R)
        small = sb("small", [P, 22, GB])
        ath = sb("ath", [P, DT, COLS], F32R)
        atl = sb("atl", [P, DT, COLS], F32R)
        RS = 4
        rr = sb("rr", [P, RS, COLS])
        rh = sb("rh", [P, HT, COLS], F32R)
        rl = sb("rl", [P, HT, COLS], F32R)
        rq = sb("rq", [P, RS, COLS])
        sums = sb("sums", [P, 2, COLS])
        ys = sb("ys", [P, 2, DI])
        yh = sb("yh", [P, 2, DI], F32R)
        yl = sb("yl", [P, 2, DI], F32R)
        resid = sb("resid", [P, GB, DI])
        t_sb = sb("t_sb", [P, GB, DI])
        bns = sb("bns", [P, GB, 6])

        p_main = [bank(f"p_main{i}") for i in range(MAIN)]
        p_at = [bank(f"p_at{i}") for i in range(2)]
        p_prep, p_agg, p_stat = bank("p_prep"), bank("p_agg"), bank("p_stat")
        prep4 = p_prep[:].rearrange("p (g c) -> p g c", g=GB)
        stat4 = p_stat[:].rearrange("p (g c) -> p g c", g=GB)
        sums4 = sums[:].rearrange("p i (g c) -> p i g c", g=GB)

        dsum, dpos, dsafe, drec, dn = (small[:, i] for i in range(5))
        deg, bpos, bsafe, brec, be = (small[:, i] for i in range(5, 10))
        mean1, msq1, var1, rstd1, sum1, sumsq1 = (small[:, i] for i in range(10, 16))
        mean2, diff2, var2, rstd2, negmean2, bias2 = (small[:, i] for i in range(16, 22))

        w1_stage = [resid[:].rearrange("p g d -> p (g d)").rearrange("p (t h) -> p t h", h=DH),
                    t_sb[:].rearrange("p g d -> p (g d)").rearrange("p (t h) -> p t h", h=DH)]
        w2_spare = sb("w2_spare", [P, HT // 2, DI])
        w2_stage = [w2_spare[:, i] for i in range(HT // 2)] + [t_sb[:, i] for i in range(HT // 2)]
        w2_beta = [rr[:, i] for i in range(RS)] + [rq[:, i] for i in range(RS)]
        beta_sum = wbb[:]
        gamma_sum, mean_weights = ys[:, 0], ys[:, 1, :P]

        consts_loaded = sem("consts_loaded")
        w1_loaded, w2_loaded = ([sem(f"{w}_loaded{i}") for i in range(2)] for w in ("w1", "w2"))
        adj_loaded, wrow_loaded, x_loaded, stored = (sem(n) for n in ("adj_loaded", "wrow_loaded", "x_loaded", "stored"))
        constants, ident_zeroed, ident_ready = sem("constants"), sem("ident_zeroed"), sem("ident_ready")
        w1h_ready, w1_ready = sem("w1h_ready"), sem("w1_ready")
        gamma_steps, w2mean_done, w2beta_done, wb_ready = (
            sem(n) for n in ("gamma_steps", "w2mean_done", "w2beta_done", "wb_ready"))
        beta_scaled, beta_steps, w2c_ready, w2h_ready = (
            sem(n) for n in ("beta_scaled", "beta_steps", "w2c_ready", "w2h_ready"))
        adjt_done, dnht_done, gt_done, at_done = sem("adjt_done"), sem("dnht_done"), sem("gt_done"), sem("at_done")
        z_done, y_done, stats_done, statsq_done, agg_done = (
            sem(n) for n in ("z_done", "y_done", "stats_done", "statsq_done", "agg_done"))
        rh_ready, r_ready, q_ready, norm_ready = sem("rh_ready"), sem("r_ready"), sem("q_ready"), sem("norm_ready")
        dnht_ready, gt_ready, gth_ready, ath_ready, yh_ready = (
            sem(n) for n in ("dnht_ready", "gt_ready", "gth_ready", "ath_ready", "yh_ready"))
        dnorm, dnh_ready, ht_ready, benorm, beht_ready = (
            sem(n) for n in ("dnorm", "dnh_ready", "ht_ready", "benorm", "beht_ready"))
        gtl_ready, atl_ready, rl_ready, sum_steps, resid_ready = (
            sem(n) for n in ("gtl_ready", "atl_ready", "rl_ready", "sum_steps", "resid_ready"))
        var1_steps, ys_ready, yl_ready, t_ready, bns_ready, var2_steps = (
            sem(n) for n in ("var1_steps", "ys_ready", "yl_ready", "t_ready", "bns_ready", "var2_steps"))
        sumsq_steps, rstd1_ready, rstd2_ready, bias2_ready, w2l_ready = (
            sem(n) for n in ("sumsq_steps", "rstd1_ready", "rstd2_ready", "bias2_ready", "w2l_ready"))

        block = ctx.enter_context(nc.Block())

        DN_STEPS, BE_STEPS, VAR1_STEPS, VAR2_STEPS = 6, 5, 7, 7
        SUM_STEPS = HT - 1

        def summed(b, ht):
            return SUM_STEPS * b + (ht + 1 if ht < 0 else max(ht, 1))

        def batches(eng, body):
            body(0, True, False)
            with nc.Fori(1, NB - 1, engines=[eng.engine], hint_back_edge=True) as b:
                body(b, False, False)
            body(NB - 1, False, True)

        @block.sync
        def _(sp):
            def load_adj(b):
                sp.dma_start(adj_sb[:], adj_v[b]).then_inc(adj_loaded, 16)
                sp.dma_start(wrow[:], w_v[b].partition_broadcast(P)).then_inc(wrow_loaded, 16)

            load_adj(0)
            for i in range(2):
                sp.dma_start(w1_stage[i], w1_v[:, 2 * i:2 * i + 2]).then_inc(w1_loaded[i], 16)
            sp.dma_start(x_sb[:], x_v[0]).then_inc(x_loaded, 16)
            for col, vec in ((b1c, b1), (gammac, gamma), (betac, beta)):
                sp.dma_start(col[:], vec).then_inc(consts_loaded, 16)
            sp.dma_start(b2b[:], b2.partition_broadcast(P)).then_inc(consts_loaded, 16)
            sp.dma_start(w2_spare[:], w2_v[:, :HT // 2]).then_inc(w2_loaded[0], 16)

            def next_adj(b):
                sp.wait_ge(dnh_ready, b)
                sp.wait_ge(adjt_done, b)
                load_adj(b)

            def next_x(b):
                sp.wait_ge(at_done, DT * b)
                sp.wait_ge(resid_ready, GB * b)
                sp.dma_start(x_sb[:], x_v[b]).then_inc(x_loaded, 16)

            def store(b):
                sp.wait_ge(norm_ready, GB * b + GB)
                sp.dma_start(out_v[b], t_sb[:]).then_inc(stored, 16)

            next_adj(1)
            sp.wait_ge(w1_ready, 1)
            sp.dma_start(t_sb[:], w2_v[:, HT // 2:]).then_inc(w2_loaded[1], 16)
            next_adj(2)
            next_x(1)
            with nc.Fori(1, NB - 2, engines=[sp.engine], hint_back_edge=True) as b:
                next_adj(b + 2)
                next_x(b + 1)
                store(b - 1)
            next_x(NB - 1)
            store(NB - 3)
            store(NB - 2)
            for g0, g1 in ((0, GB - 1), (GB - 1, GB)):
                sp.wait_ge(norm_ready, GB * (NB - 1) + g1)
                sp.dma_start(out_v[NB - 1, :, g0:g1], t_sb[:, g0:g1]).then_inc(stored, 16)
            sp.wait_ge(stored, 16 * (NB + 1))

        @block.tensor
        def _(pe):
            def transposes(src, dst, done):
                for g in range(GB):
                    last = pe.transpose(dst[:, g], src[:, g], ident[:])
                last.then_inc(done, 1)

            def prep_dnht(b, first=False):
                pe.wait_ge(dnh_ready, b + 1)
                if not first:
                    pe.wait_ge(var1_steps, VAR1_STEPS * (b - 1))
                transposes(dnh, prep4, dnht_done)

            def prep_adjt(b):
                pe.wait_ge(adj_loaded, 16 * b + 16)
                pe.wait_ge(dnht_ready, b + 1)
                transposes(adj_sb, prep4, adjt_done)

            def prep_g(b):
                pe.wait_ge(beht_ready, b + 1)
                pe.wait_ge(dnht_ready, b + 1)
                for g in range(GB):
                    last = pe.matmul(prep4[:, g], beht[:, g], dnht[:, g], start=True, stop=True)
                last.then_inc(gt_done, 1)

            def aggregate_x(b, dt, first=False):
                if dt == 0:
                    pe.wait_ge(gt_ready, b + 1)
                    pe.wait_ge(x_loaded, 16 * b + 16)
                if not (first and dt < 2):
                    pe.wait_ge(atl_ready, DT * b + dt - 1)
                for g in range(GB):
                    last = pe.matmul(p_at[dt % 2][:, g * P:(g + 1) * P], x_sb[:, g, dt * P:(dt + 1) * P],
                                     gt[:, g], start=True, stop=True)
                last.then_inc(at_done, 1)

            def hidden(b, ht, first):
                if ht < MAIN:
                    if not first:
                        pe.wait_ge(ys_ready, GB * b)
                else:
                    pe.wait_ge(r_ready, HT * b + ht - MAIN + 1)
                acc = p_main[ht % MAIN]
                for dt in range(DT):
                    if ht == 0:
                        pe.wait_ge(ath_ready, DT * b + dt + 1)
                    cols = slice(ht * P, (ht + 1) * P)
                    pe.matmul(acc[:], w1h[:, dt, cols], ath[:, dt], start=dt == 0, stop=False)
                    pe.matmul(acc[:], w1l[:, dt, cols], ath[:, dt], start=False, stop=False)
                    if ht == 0:
                        pe.wait_ge(atl_ready, DT * b + dt + 1)
                    last = pe.matmul(acc[:], w1h[:, dt, cols], atl[:, dt], start=False, stop=dt == DT - 1)
                last.then_inc(z_done, 1)

            def project(b, g, first):
                step = HT + g
                if g < GB - 1:
                    pe.wait_ge(r_ready, HT * b + step - MAIN + 1)
                else:
                    pe.wait_ge(ys_ready, GB * b + 1)
                acc = p_main[step % MAIN]
                cols = slice(g * P, (g + 1) * P)
                for ht in range(HT):
                    if g == 0:
                        pe.wait_ge(rh_ready, HT * b + ht + 1)
                        pe.wait_ge(rl_ready, HT * b + ht + 1)
                    if g == 0 and first:
                        pe.wait_ge(w2l_ready, ht + 1)
                    pe.matmul(acc[:], rh[:, ht, cols], w2h[:, ht], start=ht == 0, stop=False)
                    pe.matmul(acc[:], rh[:, ht, cols], w2l[:, ht], start=False, stop=False)
                    last = pe.matmul(acc[:], rl[:, ht, cols], w2h[:, ht], start=False, stop=ht == HT - 1)
                last.then_inc(y_done, 1)

            def statistics(b, last_batch):
                pe.wait_ge(sum_steps, SUM_STEPS * (b + 1))
                transposes(sums4[:, 0], stat4, stats_done)
                if not last_batch:
                    pe.wait_ge(gt_ready, b + 2)
                pe.wait_ge(sumsq_steps, SUM_STEPS * (b + 1))
                transposes(sums4[:, 1], prep4, statsq_done)

            def aggregate_y(b, g, first):
                if not (first and g == 0):
                    pe.wait_ge(t_ready, GB * b + g)
                if g == 0:
                    pe.wait_ge(gtl_ready, b + 1)
                pe.wait_ge(yh_ready, GB * b + g + 1)
                pe.matmul(p_agg[:], gth[:, g], yh[:, g % 2], start=True, stop=False)
                pe.matmul(p_agg[:], gtl[:, g], yh[:, g % 2], start=False, stop=False)
                pe.wait_ge(yl_ready, GB * b + g + 1)
                pe.matmul(p_agg[:], gth[:, g], yl[:, g % 2], start=False, stop=True).then_inc(agg_done, 1)

            pe.wait_ge(ident_ready, 1)
            pe.wait_ge(adj_loaded, 16)
            transposes(adj_sb, stat4, adjt_done)
            prep_dnht(0, True)
            prep_g(0)
            for dt in range(DT):
                aggregate_x(0, dt, True)

            pe.wait_ge(w1_ready, 1)

            def weight_mean():
                pe.wait_ge(constants, 3)
                pe.wait_ge(gamma_steps, HT)
                pe.matmul(p_agg[:], mean_weights, gamma_sum, start=True, stop=True).then_inc(w2mean_done, 1)

            def weight_beta():
                pe.wait_ge(beta_steps, HT - 1)
                pe.matmul(p_stat[:], ones[:], beta_sum, start=True, stop=True).then_inc(w2beta_done, 1)

            def body(b, first, last_batch):
                for ht in range(HT):
                    hidden(b, ht, first)
                    if ht == 0 and not first:
                        aggregate_y(b - 1, GB - 1, False)
                    if ht == 1 and first:
                        weight_mean()
                    if ht == 3 and first:
                        weight_beta()
                    if not last_batch:
                        if ht == 2:
                            prep_dnht(b + 1, first)
                        elif ht == 4:
                            prep_adjt(b + 1)
                        elif ht == 7:
                            prep_g(b + 1)
                for g in range(GB):
                    project(b, g, first)
                    if g == 0 and first:
                        pe.wait_ge(wb_ready, 1)
                    if g == 0:
                        statistics(b, last_batch)
                    if not last_batch:
                        aggregate_x(b + 1, g)
                    if g > 0:
                        aggregate_y(b, g - 1, first)
                if last_batch:
                    aggregate_y(b, GB - 1, False)

            batches(pe, body)

        @block.scalar
        def _(act):
            def copy_dnht(b):
                act.wait_ge(dnht_done, b + 1)
                act.activation(dnht[:], prep4, ACT.Copy).then_inc(dnht_ready, 1)

            def copy_gt(b):
                act.wait_ge(gt_done, b + 1)
                act.activation(gt[:], prep4, ACT.Copy).then_inc(gt_ready, 1)

            def split_at(b, dt):
                act.wait_ge(at_done, DT * b + dt + 1)
                act.activation(ath[:, dt], p_at[dt % 2][:], ACT.Copy).then_inc(ath_ready, 1)

            def split_w1(i):
                act.wait_ge(w1_loaded[i], 16)
                act.activation(w1h[:, 2 * i:2 * i + 2], w1_stage[i], ACT.Copy).then_inc(w1h_ready, 1)

            def split_w2(ht):
                act.wait_ge(w2c_ready, ht + 1)
                act.activation(w2h[:, ht], w2_stage[ht], ACT.Copy).then_inc(w2h_ready, 1)

            def apply_last_norm(b, g):
                act.activation(t_sb[:, g], t_sb[:, g], ACT.Identity, bias=bias2[:, g:g + 1],
                               scale=rstd2[:, g:g + 1]).then_inc(norm_ready, 1)

            def scale_by_beta(ht):
                act.wait_ge(w2_loaded[ht // (HT // 2)], 16)
                act.activation(w2_beta[ht], w2_stage[ht], ACT.Copy, scale=betac[:, ht:ht + 1]).then_inc(beta_scaled, 1)

            split_w1(0)
            copy_dnht(0)
            split_w1(1)
            copy_gt(0)
            act.wait_ge(consts_loaded, 64)
            for dt in range(DT):
                split_at(0, dt)
                scale_by_beta(dt)
            for ht in range(DT, HT):
                scale_by_beta(ht)

            def relu(b, ht, first):
                bias = b1c[:, ht:ht + 1]
                act.wait_ge(z_done, HT * b + ht + 1)
                act.activation(rh[:, ht], p_main[ht % MAIN][:], ACT.Relu, bias=bias).then_inc(rh_ready, 1)
                if first and ht < RS:
                    act.wait_ge(beta_steps, max(ht, 1))
                else:
                    act.wait_ge(rl_ready, HT * b + ht - RS + 1)
                    act.wait_ge(sum_steps, summed(b, ht - RS))
                act.activation(rr[:, ht % RS], p_main[ht % MAIN][:], ACT.Relu, bias=bias).then_inc(r_ready, 1)
                if first and ht < RS:
                    act.wait_ge(beta_steps, RS + ht)
                else:
                    act.wait_ge(sumsq_steps, summed(b, ht - RS))
                act.wait_ge(r_ready, HT * b + ht + 1)
                act.activation(rq[:, ht % RS], rr[:, ht % RS], ACT.Square).then_inc(q_ready, 1)

            def body(b, first, last_batch):
                for ht in range(HT):
                    if ht == 3 and not last_batch:
                        copy_dnht(b + 1)
                    relu(b, ht, first)
                    if ht == 1:
                        act.wait_ge(gt_ready, b + 1)
                        if not first:
                            act.wait_ge(agg_done, GB * b)
                        act.activation(gth[:], gt[:], ACT.Copy).then_inc(gth_ready, 1)
                    if first and 1 <= ht < 1 + HT // 2:
                        split_w2(2 * ht - 2)
                        split_w2(2 * ht - 1)
                    if ht == 2 and not first:
                        act.wait_ge(bias2_ready, b)
                    if 2 <= ht < 2 + GB and not first:
                        apply_last_norm(b - 1, ht - 2)
                    if not last_batch:
                        if ht == 7:
                            act.wait_ge(gtl_ready, b + 1)
                            copy_gt(b + 1)
                for g in range(GB):
                    if not last_batch:
                        split_at(b + 1, g)
                    act.wait_ge(ys_ready, GB * b + g + 1)
                    act.activation(yh[:, g % 2], ys[:, g % 2], ACT.Copy).then_inc(yh_ready, 1)
                if last_batch:
                    for g in range(GB):
                        if g == 0:
                            act.wait_ge(bias2_ready, b + 1)
                        elif g == GB - 1:
                            act.wait_ge(bias2_ready, b + 2)
                        apply_last_norm(b, g)

            batches(act, body)

        @block.vector
        def _(dve):
            def guarded_reciprocal(s, n0, total, pos, safe, rec, res):
                dve.tensor_scalar(pos, total, 0.0, None, ALU.is_gt).then_inc(s, 1)
                dve.tensor_scalar(safe, total, TINY, None, ALU.max).then_inc(s, 1)
                dve.wait_ge(s, n0 + 2)
                dve.reciprocal(rec, safe).then_inc(s, 1)
                dve.wait_ge(s, n0 + 3)
                dve.tensor_tensor(res, rec, pos, ALU.mult).then_inc(s, 1)
                dve.wait_ge(s, n0 + 4)

            def prep_dn(b, first=False):
                n = DN_STEPS * b
                dve.wait_ge(adj_loaded, 16 * b + 16)
                dve.wait_ge(wrow_loaded, 16 * b + 16)
                dve.scalar_tensor_tensor(hw[:], adj_sb[:], 0.0, wrow[:], ALU.not_equal, ALU.mult).then_inc(dnorm, 1)
                dve.wait_ge(dnorm, n + 1)
                dve.tensor_reduce(dsum, hw[:], AX.X, ALU.add).then_inc(dnorm, 1)
                dve.wait_ge(dnorm, n + 2)
                guarded_reciprocal(dnorm, n + 2, dsum, dpos, dsafe, drec, dn)
                if not first:
                    dve.wait_ge(dnht_done, b)
                for g in range(GB):
                    last = dve.tensor_scalar(dnh[:, g], adj_sb[:, g], 0.0, dn[:, g:g + 1], ALU.not_equal, ALU.mult)
                last.then_inc(dnh_ready, 1)

            def prep_be(b, first=False, source=prep4):
                n = BE_STEPS * b
                dve.wait_ge(adjt_done, b + 1)
                dve.tensor_scalar(ht_sb[:], source, 0.0, None, ALU.not_equal).then_inc(ht_ready, 1)
                dve.wait_ge(ht_ready, b + 1)
                dve.tensor_reduce(deg, ht_sb[:], AX.X, ALU.add).then_inc(benorm, 1)
                dve.wait_ge(benorm, n + 1)
                guarded_reciprocal(benorm, n + 1, deg, bpos, bsafe, brec, be)
                if not first:
                    dve.wait_ge(gt_done, b)
                for g in range(GB):
                    last = dve.tensor_scalar(beht[:, g], ht_sb[:, g], be[:, g:g + 1], None, ALU.mult)
                last.then_inc(beht_ready, 1)

            def split_at(b, dt):
                dve.wait_ge(ath_ready, DT * b + dt + 1)
                dve.tensor_tensor(atl[:, dt], p_at[dt % 2][:], ath[:, dt].bitcast(F32), ALU.subtract)\
                   .then_inc(atl_ready, 1)

            def add_gamma(ht):
                dve.wait_ge(w2_loaded[ht // (HT // 2)], 16)
                if ht == 0:
                    dve.tensor_scalar(gamma_sum, w2_stage[ht], gammac[:, ht:ht + 1], None, ALU.mult)\
                       .then_inc(gamma_steps, 1)
                else:
                    dve.wait_ge(gamma_steps, ht)
                    dve.scalar_tensor_tensor(gamma_sum, w2_stage[ht], gammac[:, ht:ht + 1], gamma_sum,
                                             ALU.mult, ALU.add).then_inc(gamma_steps, 1)

            dve.memset(ones[:], 1.0).then_inc(constants, 1)
            dve.memset(mean_weights, 1.0 / DH).then_inc(constants, 1)
            dve.memset(neghalf[:], -0.5).then_inc(constants, 1)
            prep_dn(0, True)
            prep_be(0, True, stat4)
            for i in range(2):
                dve.wait_ge(w1h_ready, i + 1)
                last = dve.tensor_tensor(w1l[:, 2 * i:2 * i + 2], w1_stage[i], w1h[:, 2 * i:2 * i + 2].bitcast(F32),
                                         ALU.subtract)
            last.then_inc(w1_ready, 1)
            dve.wait_ge(consts_loaded, 64)
            for dt in range(DT):
                split_at(0, dt)
                add_gamma(dt)
            for ht in range(DT, HT):
                add_gamma(ht)

            def centre_w2(ht):
                if ht == 0:
                    dve.wait_ge(beta_scaled, HT)
                    dve.wait_ge(w2mean_done, 1)
                dve.scalar_tensor_tensor(w2_stage[ht], w2_stage[ht], gammac[:, ht:ht + 1], p_agg[:],
                                         ALU.mult, ALU.subtract).then_inc(w2c_ready, 1)

            def residual(b, g):
                dve.wait_ge(x_loaded, 16 * b + 16)
                dve.scalar_tensor_tensor(resid[:, g], x_sb[:, g], 2.0, b2b[:], ALU.mult, ALU.add)\
                   .then_inc(resid_ready, 1)

            def first_norm(b):
                n = VAR1_STEPS * b
                dve.wait_ge(stats_done, b + 1)
                dve.tensor_reduce(sum1, stat4, AX.X, ALU.add).then_inc(var1_steps, 1)
                dve.wait_ge(var1_steps, n + 1)
                dve.tensor_scalar(mean1, sum1, 1.0 / DH, None, ALU.mult).then_inc(var1_steps, 1)
                dve.wait_ge(var1_steps, n + 2)
                dve.tensor_tensor(msq1, mean1, mean1, ALU.mult).then_inc(var1_steps, 1)
                dve.wait_ge(statsq_done, b + 1)
                dve.tensor_reduce(sumsq1, prep4, AX.X, ALU.add).then_inc(var1_steps, 1)
                dve.wait_ge(var1_steps, n + 4)
                dve.tensor_scalar(var1, sumsq1, 1.0 / DH, EPS, ALU.mult, ALU.add).then_inc(var1_steps, 1)
                dve.wait_ge(var1_steps, n + 5)
                dve.tensor_tensor(var1, var1, msq1, ALU.subtract).then_inc(var1_steps, 1)
                dve.wait_ge(var1_steps, n + 6)
                dve.tensor_scalar(var1, var1, EPS, None, ALU.max).then_inc(var1_steps, 1)

            def normalised(b, g):
                if g == 0:
                    dve.wait_ge(rstd1_ready, b + 1)
                dve.wait_ge(y_done, GB * b + g + 1)
                dve.scalar_tensor_tensor(ys[:, g % 2], p_main[(HT + g) % MAIN][:], rstd1[:, g:g + 1], wbb[:],
                                         ALU.mult, ALU.add).then_inc(ys_ready, 1)

            def split_y(b, g):
                dve.wait_ge(yh_ready, GB * b + g + 1)
                dve.tensor_tensor(yl[:, g % 2], ys[:, g % 2], yh[:, g % 2].bitcast(F32), ALU.subtract)\
                   .then_inc(yl_ready, 1)

            def add_residual(b, g, first):
                if g == 0 and not first:
                    dve.wait_ge(stored, 16 * b)
                dve.wait_ge(agg_done, GB * b + g + 1)
                dve.tensor_tensor(t_sb[:, g], p_agg[:], resid[:, g], ALU.add).then_inc(t_ready, 1)

            def result_statistics(b, g):
                dve.wait_ge(t_ready, GB * b + g + 1)
                dve.bn_stats(bns[:, g], t_sb[:, g]).then_inc(bns_ready, 1)

            def last_norm(b, g0=0, g1=GB, part=0):
                dve.wait_ge(bns_ready, GB * b + g1)
                n = VAR2_STEPS * (b + part)
                mean_even, m2_even, mean_odd, m2_odd = (bns[:, g0:g1, i] for i in (1, 2, 4, 5))
                graphs = slice(g0, g1)
                dve.tensor_tensor(mean2[:, graphs], mean_even, mean_odd, ALU.add).then_inc(var2_steps, 1)
                dve.tensor_tensor(diff2[:, graphs], mean_even, mean_odd, ALU.subtract).then_inc(var2_steps, 1)
                dve.tensor_tensor(var2[:, graphs], m2_even, m2_odd, ALU.add).then_inc(var2_steps, 1)
                dve.wait_ge(var2_steps, n + 3)
                dve.tensor_scalar(negmean2[:, graphs], mean2[:, graphs], -0.5, None, ALU.mult).then_inc(var2_steps, 1)
                dve.scalar_tensor_tensor(diff2[:, graphs], diff2[:, graphs], 0.25, diff2[:, graphs],
                                         ALU.mult, ALU.mult).then_inc(var2_steps, 1)
                dve.tensor_scalar(var2[:, graphs], var2[:, graphs], 1.0 / DI, EPS,
                                  ALU.mult, ALU.add).then_inc(var2_steps, 1)
                dve.wait_ge(var2_steps, n + 6)
                dve.tensor_tensor(var2[:, graphs], var2[:, graphs], diff2[:, graphs], ALU.add).then_inc(var2_steps, 1)

            def add_tile(b, ht):
                if ht == 1:
                    dve.tensor_tensor(sums[:, 0], rr[:, 0], rr[:, 1], ALU.add).then_inc(sum_steps, 1)
                elif ht > 1:
                    dve.wait_ge(sum_steps, SUM_STEPS * b + ht - 1)
                    dve.tensor_tensor(sums[:, 0], sums[:, 0], rr[:, ht % RS], ALU.add).then_inc(sum_steps, 1)

            def body(b, first, last_batch):
                if not last_batch:
                    prep_dn(b + 1)
                for ht in range(HT):
                    dve.wait_ge(r_ready, HT * b + ht + 1)
                    dve.tensor_tensor(rl[:, ht], rr[:, ht % RS], rh[:, ht].bitcast(F32), ALU.subtract)\
                       .then_inc(rl_ready, 1)
                    if ht == 0 and not first:
                        add_residual(b - 1, GB - 1, False)
                        result_statistics(b - 1, GB - 1)
                        last_norm(b - 1)
                        residual(b, GB - 1)
                    add_tile(b, ht)
                    if first and ht < HT // 2:
                        centre_w2(2 * ht)
                        centre_w2(2 * ht + 1)
                    if ht < GB and first:
                        residual(b, ht)
                    if ht == 4 and not last_batch:
                        prep_be(b + 1)
                    if ht == 5 and first:
                        dve.wait_ge(w2beta_done, 1)
                        dve.tensor_copy(wbb[:], p_stat[:]).then_inc(wb_ready, 1)
                first_norm(b)
                if first:
                    dve.wait_ge(wb_ready, 1)
                for g in range(GB):
                    if g == 0 and not last_batch:
                        split_at(b + 1, g)
                    normalised(b, g)
                    if g > 0:
                        if not last_batch:
                            split_at(b + 1, g)
                        add_residual(b, g - 1, first)
                    split_y(b, g)
                    if g > 0:
                        result_statistics(b, g - 1)
                    if last_batch and g == GB - 1:
                        last_norm(b, 0, GB - 1)
                    if not last_batch:
                        if g > 0:
                            residual(b + 1, g - 1)
                if last_batch:
                    add_residual(b, GB - 1, False)
                    result_statistics(b, GB - 1)
                    last_norm(b, GB - 1, GB, 1)

            batches(dve, body)

        @block.gpsimd
        def _(pool):
            pool.memset(ident[:], 0.0).then_inc(ident_zeroed, 1)
            pool.wait_ge(ident_zeroed, 1)
            pool.affine_select(out=ident[:], in_=ident[:], compare_op=ALU.not_equal, fill=1.0, base=0,
                               pattern=[[-1, P]], channel_multiplier=1).then_inc(ident_ready, 1)

            def root2(b, g0=0, g1=GB, part=0):
                graphs = slice(g0, g1)
                pool.wait_ge(var2_steps, VAR2_STEPS * (b + part + 1))
                pool.tensor_tensor(rstd2[:, graphs], var2[:, graphs], neghalf[:, graphs], ALU.pow)\
                    .then_inc(rstd2_ready, 1)
                pool.wait_ge(rstd2_ready, b + part + 1)
                pool.tensor_tensor(bias2[:, graphs], negmean2[:, graphs], rstd2[:, graphs], ALU.mult)\
                    .then_inc(bias2_ready, 1)

            pool.wait_ge(beta_scaled, 1)
            for ht in range(1, HT):
                pool.wait_ge(beta_scaled, ht + 1)
                if ht > 1:
                    pool.wait_ge(beta_steps, ht - 1)
                so_far = w2_beta[0] if ht == 1 else beta_sum
                pool.tensor_tensor(beta_sum, so_far, w2_beta[ht], ALU.add).then_inc(beta_steps, 1)

            def split_w2(ht):
                pool.wait_ge(w2h_ready, ht + 1)
                pool.tensor_tensor(w2l[:, ht], w2_stage[ht], w2h[:, ht].bitcast(F32), ALU.subtract)\
                    .then_inc(w2l_ready, 1)

            def body(b, first, last_batch):
                if not first:
                    root2(b - 1)
                pool.wait_ge(gth_ready, b + 1)
                pool.tensor_tensor(gtl[:], gt[:], gth[:].bitcast(F32), ALU.subtract).then_inc(gtl_ready, 1)
                for ht in range(1, HT):
                    pool.wait_ge(q_ready, HT * b + ht + 1)
                    if ht == 1:
                        pool.tensor_tensor(sums[:, 1], rq[:, 0], rq[:, 1], ALU.add).then_inc(sumsq_steps, 1)
                    else:
                        pool.wait_ge(sumsq_steps, SUM_STEPS * b + ht - 1)
                        pool.tensor_tensor(sums[:, 1], sums[:, 1], rq[:, ht % RS], ALU.add).then_inc(sumsq_steps, 1)
                    if first and ht < 1 + HT // 2:
                        split_w2(2 * ht - 2)
                        split_w2(2 * ht - 1)
                pool.wait_ge(var1_steps, VAR1_STEPS * (b + 1))
                pool.tensor_tensor(rstd1, var1, neghalf[:], ALU.pow).then_inc(rstd1_ready, 1)
                if last_batch:
                    root2(b, 0, GB - 1)
                    root2(b, GB - 1, GB, 1)

            batches(pool, body)


_INS = ["x", "adj", "w1t", "b1", "gamma", "beta", "w2t", "b2"]


def kernel(x, adj, L0_gnn_W1, L0_gnn_b1, L0_gnn_gamma, L0_gnn_beta, L0_gnn_W2, L0_gnn_b2):
    import numpy as np
    import concourse.bacc as bacc
    from concourse.bass_utils import run_bass_kernel_spmd

    def tiles(vector):
        return np.asarray(vector).reshape(-1, P).T

    given = dict(zip(_INS, (x, adj, np.asarray(L0_gnn_W1).T, tiles(L0_gnn_b1), tiles(L0_gnn_gamma),
                            tiles(L0_gnn_beta), np.asarray(L0_gnn_W2).T, L0_gnn_b2)))
    nc = bacc.Bacc("TRN2", target_bir_lowering=False, num_devices=1)
    arrays, args = {}, []
    for name, a in given.items():
        a = np.ascontiguousarray(a)
        arrays[name] = a
        args.append(nc.dram_tensor(name, a.shape, mybir.dt.from_np(a.dtype), kind="ExternalInput").ap())
    args.append(nc.dram_tensor("out", x.shape, F32, kind="ExternalOutput").ap())
    adj_resnorm_kernel(nc, *args)
    r = run_bass_kernel_spmd(nc, [arrays], core_ids=[0])
    return r.results[0]["out"]
```
